# Optimizing a Trainium2 kernel written in Bass

```python
import numpy as np
import jax
import jax.numpy as jnp

def _softmax(x, axis=-1):
    return jax.nn.softmax(x, axis=axis)

def _gelu(x):
    return jax.nn.gelu(x, approximate=True)

def _silu(x):
    return jax.nn.silu(x)

def _sigmoid(x):
    return jax.nn.sigmoid(x)

def _layernorm(x, axis=-1, eps=1e-05):
    m = jnp.mean(x, axis=axis, keepdims=True)
    v = jnp.var(x, axis=axis, keepdims=True)
    return (x - m) / jnp.sqrt(v + eps)

def _scatter_add(tgt, idx, src, axis=0):
    return tgt.at[idx].add(src)

def _segment_sum(src, seg, n):
    return jax.ops.segment_sum(src, seg, n)
kernel_name = 'mk_dlrm_tower_d1_rec_r8_79d60f'

def setup_inputs(seed: int=0):
    np.random.seed(seed)
    _w = jnp.asarray

    def _rec_inputs():
        import jax
        import jax.numpy as jnp
        _tk = jax.random.key(seed)
        dense_ctx = jax.random.normal(jax.random.fold_in(_tk, 190), (2048, 16), jnp.float32)
        ids = jnp.stack([jax.random.randint(jax.random.fold_in(_tk, 200 + f), (2048,), 0, v, jnp.int32) for f, v in enumerate([125000, 12500, 1250, 125000, 125000, 1000, 125000, 1250, 1250, 12500, 1000, 1000, 12500, 125000, 1000, 1250, 1250, 125000, 125000, 1250, 1000, 1000, 12500, 1000, 1250, 12500, 12500, 1250, 12500, 1000, 1000, 1000, 1000, 1250, 1000, 1000, 1000, 1000, 1000, 1000])], axis=1)
        tbl_0 = 0.05 * jax.random.normal(jax.random.fold_in(_tk, 500 + 0), (125000, 32), jnp.float32)
        tbl_1 = 0.05 * jax.random.normal(jax.random.fold_in(_tk, 500 + 1), (12500, 32), jnp.float32)
        tbl_2 = 0.05 * jax.random.normal(jax.random.fold_in(_tk, 500 + 2), (1250, 32), jnp.float32)
        tbl_3 = 0.05 * jax.random.normal(jax.random.fold_in(_tk, 500 + 3), (125000, 32), jnp.float32)
        tbl_4 = 0.05 * jax.random.normal(jax.random.fold_in(_tk, 500 + 4), (125000, 32), jnp.float32)
        tbl_5 = 0.05 * jax.random.normal(jax.random.fold_in(_tk, 500 + 5), (1000, 32), jnp.float32)
        tbl_6 = 0.05 * jax.random.normal(jax.random.fold_in(_tk, 500 + 6), (125000, 32), jnp.float32)
        tbl_7 = 0.05 * jax.random.normal(jax.random.fold_in(_tk, 500 + 7), (1250, 32), jnp.float32)
        tbl_8 = 0.05 * jax.random.normal(jax.random.fold_in(_tk, 500 + 8), (1250, 32), jnp.float32)
        tbl_9 = 0.05 * jax.random.normal(jax.random.fold_in(_tk, 500 + 9), (12500, 32), jnp.float32)
        tbl_10 = 0.05 * jax.random.normal(jax.random.fold_in(_tk, 500 + 10), (1000, 32), jnp.float32)
        tbl_11 = 0.05 * jax.random.normal(jax.random.fold_in(_tk, 500 + 11), (1000, 32), jnp.float32)
        tbl_12 = 0.05 * jax.random.normal(jax.random.fold_in(_tk, 500 + 12), (12500, 32), jnp.float32)
        tbl_13 = 0.05 * jax.random.normal(jax.random.fold_in(_tk, 500 + 13), (125000, 32), jnp.float32)
        tbl_14 = 0.05 * jax.random.normal(jax.random.fold_in(_tk, 500 + 14), (1000, 32), jnp.float32)
        tbl_15 = 0.05 * jax.random.normal(jax.random.fold_in(_tk, 500 + 15), (1250, 32), jnp.float32)
        tbl_16 = 0.05 * jax.random.normal(jax.random.fold_in(_tk, 500 + 16), (1250, 32), jnp.float32)
        tbl_17 = 0.05 * jax.random.normal(jax.random.fold_in(_tk, 500 + 17), (125000, 32), jnp.float32)
        tbl_18 = 0.05 * jax.random.normal(jax.random.fold_in(_tk, 500 + 18), (125000, 32), jnp.float32)
        tbl_19 = 0.05 * jax.random.normal(jax.random.fold_in(_tk, 500 + 19), (1250, 32), jnp.float32)
        tbl_20 = 0.05 * jax.random.normal(jax.random.fold_in(_tk, 500 + 20), (1000, 32), jnp.float32)
        tbl_21 = 0.05 * jax.random.normal(jax.random.fold_in(_tk, 500 + 21), (1000, 32), jnp.float32)
        tbl_22 = 0.05 * jax.random.normal(jax.random.fold_in(_tk, 500 + 22), (12500, 32), jnp.float32)
        tbl_23 = 0.05 * jax.random.normal(jax.random.fold_in(_tk, 500 + 23), (1000, 32), jnp.float32)
        tbl_24 = 0.05 * jax.random.normal(jax.random.fold_in(_tk, 500 + 24), (1250, 32), jnp.float32)
        tbl_25 = 0.05 * jax.random.normal(jax.random.fold_in(_tk, 500 + 25), (12500, 32), jnp.float32)
        tbl_26 = 0.05 * jax.random.normal(jax.random.fold_in(_tk, 500 + 26), (12500, 32), jnp.float32)
        tbl_27 = 0.05 * jax.random.normal(jax.random.fold_in(_tk, 500 + 27), (1250, 32), jnp.float32)
        tbl_28 = 0.05 * jax.random.normal(jax.random.fold_in(_tk, 500 + 28), (12500, 32), jnp.float32)
        tbl_29 = 0.05 * jax.random.normal(jax.random.fold_in(_tk, 500 + 29), (1000, 32), jnp.float32)
        tbl_30 = 0.05 * jax.random.normal(jax.random.fold_in(_tk, 500 + 30), (1000, 32), jnp.float32)
        tbl_31 = 0.05 * jax.random.normal(jax.random.fold_in(_tk, 500 + 31), (1000, 32), jnp.float32)
        tbl_32 = 0.05 * jax.random.normal(jax.random.fold_in(_tk, 500 + 32), (1000, 32), jnp.float32)
        tbl_33 = 0.05 * jax.random.normal(jax.random.fold_in(_tk, 500 + 33), (1250, 32), jnp.float32)
        tbl_34 = 0.05 * jax.random.normal(jax.random.fold_in(_tk, 500 + 34), (1000, 32), jnp.float32)
        tbl_35 = 0.05 * jax.random.normal(jax.random.fold_in(_tk, 500 + 35), (1000, 32), jnp.float32)
        tbl_36 = 0.05 * jax.random.normal(jax.random.fold_in(_tk, 500 + 36), (1000, 32), jnp.float32)
        tbl_37 = 0.05 * jax.random.normal(jax.random.fold_in(_tk, 500 + 37), (1000, 32), jnp.float32)
        tbl_38 = 0.05 * jax.random.normal(jax.random.fold_in(_tk, 500 + 38), (1000, 32), jnp.float32)
        tbl_39 = 0.05 * jax.random.normal(jax.random.fold_in(_tk, 500 + 39), (1000, 32), jnp.float32)
        _rk = jax.random.fold_in(_tk, 7)
        W_top1 = 0.176777 * jax.random.normal(jax.random.fold_in(_tk, 801), (32, 512), jnp.float32)
        W_top2 = 0.0441942 * jax.random.normal(jax.random.fold_in(_tk, 802), (512, 256), jnp.float32)
        W_top3 = 0.0625 * jax.random.normal(jax.random.fold_in(_tk, 803), (256, 1), jnp.float32)
        b_top1 = jnp.zeros((512,), jnp.float32)
        b_top2 = jnp.zeros((256,), jnp.float32)
        return (dense_ctx, ids, tbl_0, tbl_1, tbl_2, tbl_3, tbl_4, tbl_5, tbl_6, tbl_7, tbl_8, tbl_9, tbl_10, tbl_11, tbl_12, tbl_13, tbl_14, tbl_15, tbl_16, tbl_17, tbl_18, tbl_19, tbl_20, tbl_21, tbl_22, tbl_23, tbl_24, tbl_25, tbl_26, tbl_27, tbl_28, tbl_29, tbl_30, tbl_31, tbl_32, tbl_33, tbl_34, tbl_35, tbl_36, tbl_37, tbl_38, tbl_39, W_top1, b_top1, W_top2, b_top2, W_top3)
    dense_ctx, ids, tbl_0, tbl_1, tbl_2, tbl_3, tbl_4, tbl_5, tbl_6, tbl_7, tbl_8, tbl_9, tbl_10, tbl_11, tbl_12, tbl_13, tbl_14, tbl_15, tbl_16, tbl_17, tbl_18, tbl_19, tbl_20, tbl_21, tbl_22, tbl_23, tbl_24, tbl_25, tbl_26, tbl_27, tbl_28, tbl_29, tbl_30, tbl_31, tbl_32, tbl_33, tbl_34, tbl_35, tbl_36, tbl_37, tbl_38, tbl_39, W_top1, b_top1, W_top2, b_top2, W_top3 = _rec_inputs()

    def _L0_rec_setup():
        import jax, jax.numpy as jnp
        import numpy as np
        import itertools
        LN_EPS = 0.001

        def _pair_indices(field_num):
            pairs = np.array(list(itertools.combinations(range(field_num), 2)), dtype=np.int32)
            return (pairs[:, 0], pairs[:, 1])
        key = jax.random.key(seed)
        ks = jax.random.split(key, 3)
        B, F, E, P, D = (256, 40, 32, 780, 16)
        x = jax.random.normal(ks[0], (B, F, E), dtype=jnp.float32)
        W = jax.random.normal(ks[1], (P, E, E), dtype=jnp.float32) * (2.0 / (E + E)) ** 0.5
        dense_w = jax.random.normal(ks[2], (P, D), dtype=jnp.float32) * (2.0 / (P + D)) ** 0.5
        dense_b = jnp.zeros((D,), dtype=jnp.float32)
        gamma = jnp.ones((D,), dtype=jnp.float32)
        beta = jnp.zeros((D,), dtype=jnp.float32)
        return {'x': x, 'W': W, 'dense_w': dense_w, 'dense_b': dense_b, 'gamma': gamma, 'beta': beta}
    _L0_rec_all = _L0_rec_setup()
    _L0_rec_in = {k: v for k, v in _L0_rec_all.items() if k in ('W', 'dense_w', 'dense_b', 'gamma', 'beta')}
    del _L0_rec_all
    return {'dense_ctx': dense_ctx, 'ids': ids, 'tbl_0': tbl_0, 'tbl_1': tbl_1, 'tbl_2': tbl_2, 'tbl_3': tbl_3, 'tbl_4': tbl_4, 'tbl_5': tbl_5, 'tbl_6': tbl_6, 'tbl_7': tbl_7, 'tbl_8': tbl_8, 'tbl_9': tbl_9, 'tbl_10': tbl_10, 'tbl_11': tbl_11, 'tbl_12': tbl_12, 'tbl_13': tbl_13, 'tbl_14': tbl_14, 'tbl_15': tbl_15, 'tbl_16': tbl_16, 'tbl_17': tbl_17, 'tbl_18': tbl_18, 'tbl_19': tbl_19, 'tbl_20': tbl_20, 'tbl_21': tbl_21, 'tbl_22': tbl_22, 'tbl_23': tbl_23, 'tbl_24': tbl_24, 'tbl_25': tbl_25, 'tbl_26': tbl_26, 'tbl_27': tbl_27, 'tbl_28': tbl_28, 'tbl_29': tbl_29, 'tbl_30': tbl_30, 'tbl_31': tbl_31, 'tbl_32': tbl_32, 'tbl_33': tbl_33, 'tbl_34': tbl_34, 'tbl_35': tbl_35, 'tbl_36': tbl_36, 'tbl_37': tbl_37, 'tbl_38': tbl_38, 'tbl_39': tbl_39, 'W_top1': W_top1, 'b_top1': b_top1, 'W_top2': W_top2, 'b_top2': b_top2, 'W_top3': W_top3, 'L0_rec_W': _L0_rec_in['W'], 'L0_rec_dense_w': _L0_rec_in['dense_w'], 'L0_rec_dense_b': _L0_rec_in['dense_b'], 'L0_rec_gamma': _L0_rec_in['gamma'], 'L0_rec_beta': _L0_rec_in['beta']}

def reference(dense_ctx, ids, tbl_0, tbl_1, tbl_2, tbl_3, tbl_4, tbl_5, tbl_6, tbl_7, tbl_8, tbl_9, tbl_10, tbl_11, tbl_12, tbl_13, tbl_14, tbl_15, tbl_16, tbl_17, tbl_18, tbl_19, tbl_20, tbl_21, tbl_22, tbl_23, tbl_24, tbl_25, tbl_26, tbl_27, tbl_28, tbl_29, tbl_30, tbl_31, tbl_32, tbl_33, tbl_34, tbl_35, tbl_36, tbl_37, tbl_38, tbl_39, W_top1, b_top1, W_top2, b_top2, W_top3, L0_rec_W, L0_rec_dense_w, L0_rec_dense_b, L0_rec_gamma, L0_rec_beta):
    import jax
    import jax.numpy as jnp

    def _L0_rec_ref(x, W, dense_w, dense_b, gamma, beta):
        import jax, jax.numpy as jnp
        import numpy as np
        import itertools
        LN_EPS = 0.001

        def _pair_indices(field_num):
            pairs = np.array(list(itertools.combinations(range(field_num), 2)), dtype=np.int32)
            return (pairs[:, 0], pairs[:, 1])
        F = x.shape[1]
        idx_i, idx_j = _pair_indices(F)
        xi = x[:, idx_i, :]
        xj = x[:, idx_j, :]
        t = jnp.einsum('bpe,pef->bpf', xi, W)
        p = jnp.einsum('bpf,bpf->bp', t, xj)
        h = p @ dense_w + dense_b
        mu = jnp.mean(h, axis=-1, keepdims=True)
        var = jnp.mean(jnp.square(h - mu), axis=-1, keepdims=True)
        out = (h - mu) * jax.lax.rsqrt(var + LN_EPS) * gamma + beta
        return out
    e = jnp.stack([tbl_0[ids[:, 0]], tbl_1[ids[:, 1]], tbl_2[ids[:, 2]], tbl_3[ids[:, 3]], tbl_4[ids[:, 4]], tbl_5[ids[:, 5]], tbl_6[ids[:, 6]], tbl_7[ids[:, 7]], tbl_8[ids[:, 8]], tbl_9[ids[:, 9]], tbl_10[ids[:, 10]], tbl_11[ids[:, 11]], tbl_12[ids[:, 12]], tbl_13[ids[:, 13]], tbl_14[ids[:, 14]], tbl_15[ids[:, 15]], tbl_16[ids[:, 16]], tbl_17[ids[:, 17]], tbl_18[ids[:, 18]], tbl_19[ids[:, 19]], tbl_20[ids[:, 20]], tbl_21[ids[:, 21]], tbl_22[ids[:, 22]], tbl_23[ids[:, 23]], tbl_24[ids[:, 24]], tbl_25[ids[:, 25]], tbl_26[ids[:, 26]], tbl_27[ids[:, 27]], tbl_28[ids[:, 28]], tbl_29[ids[:, 29]], tbl_30[ids[:, 30]], tbl_31[ids[:, 31]], tbl_32[ids[:, 32]], tbl_33[ids[:, 33]], tbl_34[ids[:, 34]], tbl_35[ids[:, 35]], tbl_36[ids[:, 36]], tbl_37[ids[:, 37]], tbl_38[ids[:, 38]], tbl_39[ids[:, 39]]], axis=1)
    z = _L0_rec_ref(e, L0_rec_W, L0_rec_dense_w, L0_rec_dense_b, L0_rec_gamma, L0_rec_beta)
    z = z.reshape(z.shape[0], -1)
    h = jnp.concatenate([z, dense_ctx], axis=1)
    h = jnp.maximum(h @ W_top1 + b_top1, 0.0)
    h = jnp.maximum(h @ W_top2 + b_top2, 0.0)
    y = h @ W_top3
    return y

_drawn_inputs = setup_inputs


def setup_inputs(seed=0):
    import zlib

    import numpy as np

    out = dict(_drawn_inputs(seed))
    spreads = {'b_top1': (0.0, 0.1),
     'b_top2': (0.0, 0.1),
     'L0_rec_dense_b': (0.0, 0.1),
     'L0_rec_gamma': (1.0, 0.2),
     'L0_rec_beta': (0.0, 0.1)}
    factors = {}
    for name, (base, spread) in spreads.items():
        noise = np.random.default_rng([zlib.crc32(name.encode()), seed]).standard_normal(out[name].shape)
        drawn = base * np.exp(spread * noise) if base else spread * noise
        out[name] = jnp.asarray(drawn.astype(out[name].dtype))
    for name, factor in factors.items():
        out[name] = (out[name] * factor).astype(out[name].dtype)
    return out
```

```python
from contextlib import ExitStack

import concourse.bass as bass
from concourse import mybir

F32 = mybir.dt.float32
BF16 = mybir.dt.bfloat16
I32 = mybir.dt.int32
ALU = mybir.AluOpType
ACT = mybir.ActivationFunctionType
AX_X = mybir.AxisListType.X

P = 128
BATCH = 2048
FIELDS = 40
E = 32
D = 16
CH = 512
NCH = BATCH // CH
BT = CH // P
R = P // E
NC = FIELDS // R
NQ = NC * (NC + 1) // 2
H1, H2 = 512, 256
K1 = H1 // P
K2 = H2 // P
LN_EPS = 1e-3

GROUP = 2
T_SLOTS = 3
Q_SLOTS = 4
W_ROUND = 8
W_ROUNDS = [(q, min(q + W_ROUND, NQ)) for q in range(0, NQ, W_ROUND)]


def pair_slot(a, c):
    return c * (c + 1) // 2 + a


def step_groups(c):
    tiles = [(a, r) for a in range(c + 1) for r in range(R) if not (a == c and r == R - 1)]
    return [tiles[n:n + GROUP] for n in range(0, len(tiles), GROUP)]


GROUPS = [(c, tiles) for c in range(NC) for tiles in step_groups(c)]
NG = len(GROUPS)
STEP_END = [max(n for n, g in enumerate(GROUPS) if g[0] == c) + 1 for c in range(NC)]
LAST_USE = [max(n for n, (_, tiles) in enumerate(GROUPS) if any(a == b for a, _ in tiles)) for b in range(NC)]
STEP_START = [0] + STEP_END[:-1]
BATCHES = [list(range(n, min(n + 2, NG))) for n in range(0, NG, 2)]
NBATCH = len(BATCHES)
BATCH_OF = {g: n for n, b in enumerate(BATCHES) for g in b}


def build(nc, ids, ctx_in, W_in, dw_in, w1_in, w2_in, w3_in, b2_in, rows_in, ident_in, sel_in, *rest):
    tables, out = rest[:FIELDS], rest[FIELDS]

    with ExitStack() as ctx:
        def sb(name, shape, dt):
            return ctx.enter_context(nc.sbuf_tensor(name, shape, dt))

        def sem(name):
            return ctx.enter_context(nc.semaphore(name))

        w_a = sb("w_a", [P, R, NQ, P], BF16)
        w_b = sb("w_b", [P, R // 2, NQ, P], BF16)
        x_a = sb("x_a", [P, NC, R, CH], BF16)
        x_b = sb("x_b", [P, NC, R // 2, CH], BF16)
        dw = sb("dw", [P, R, NQ, D], F32)
        q_buf = sb("q_buf", [P, Q_SLOTS, GROUP, CH], F32)
        xt = sb("xt", [P, 2, CH], F32)
        rows = sb("rows", [P, 2, BT, P], F32)
        parts = sb("parts", [P, 2, 3, CH], BF16)
        ids_all = sb("ids_all", [P, NCH, FIELDS * BT], I32)
        ident = sb("ident", [P, P], F32)
        neg_ident = sb("neg_ident", [P, P], BF16)
        sel = sb("sel", [P, D], F32)
        w1 = sb("w1", [E + 1, H1], F32)
        w2 = sb("w2", [P, K1, H2], F32)
        w3 = sb("w3", [P, K2], F32)
        b2 = sb("b2", [P, K2], F32)
        row_consts = sb("row_consts", [P, 3, D], F32)
        h_parts = sb("h_parts", [P, CH], F32)
        h_sb = sb("h_sb", [P, BT, D], F32)
        sq = sb("sq", [P, BT, D], F32)
        stat = sb("stat", [P, 3, BT], F32)
        zc = sb("zc", [P, BT, P], F32)
        zct = sb("zct", [E + 1, CH], F32)
        y_sb = sb("y_sb", [1, CH], F32)
        hid1 = q_buf[:, 0:2, :, :].rearrange("p s g b -> p (s g) b")
        hid2 = q_buf[:, 2, :, :]
        stage = x_a[:, NC // 2:NC, :, :].rearrange("p c r b -> p (c r b)")
        SZ = W_ROUND * P

        def w_full(n):
            return stage[:, (n % 2) * 5 * SZ:(n % 2) * 5 * SZ + 2 * SZ].bitcast(F32)

        def w_parts(n):
            return stage[:, (n % 2) * 5 * SZ + 2 * SZ:(n % 2) * 5 * SZ + 5 * SZ].rearrange("p (s n) -> p s n", s=3)

        t_ps = ctx.enter_context(nc.psum_tensor("t_ps", [P, T_SLOTS * GROUP, CH], F32))
        turn_ps = ctx.enter_context(nc.psum_tensor("turn_ps", [P, CH], F32))
        h_ps = ctx.enter_context(nc.psum_tensor("h_ps", [P, CH], F32))
        sum_ps = t_ps[:, 0, 0:BT * D]
        zct_ps = t_ps[:, 1, :]
        y_ps = t_ps[0:1, 2, :]

        w_spill = nc.dram_tensor("w_spill", [3, E, R, NQ * P], BF16, kind="Internal").ap()
        x_spill = nc.dram_tensor("x_spill", [2, 3, E, R, CH], BF16, kind="Internal").ap()

        ids_in = sem("ids_in")
        consts_in = sem("consts_in")
        w_in = [sem(f"w_in{n}") for n in range(2)]
        w_high, w_rest, w_mid, w_low = sem("w_high"), sem("w_rest"), sem("w_mid"), sem("w_low")
        w_spilled = sem("w_spilled")
        w_stacked = [sem(f"w_stacked{n}") for n in range(len(W_ROUNDS))]
        neg_made = sem("neg_made")
        ones_made = sem("ones_made")
        h_cleared = sem("h_cleared")
        gathered = [sem(f"gathered{n}") for n in range(2)]
        turned = sem("turned")
        xt_ready = sem("xt_ready")
        high_ready = sem("high_ready")
        less_high = sem("less_high")
        mid_ready = sem("mid_ready")
        less_mid = sem("less_mid")
        parts_ready = sem("parts_ready")
        spilled = sem("spilled")
        x_stacked = [sem(f"x_stacked{n}") for n in range(2)]
        t_ready = sem("t_ready")
        multiplied = sem("multiplied")
        summed = sem("summed")
        h_taken = sem("h_taken")
        sum_ready = sem("sum_ready")
        ln_step = sem("ln_step")
        var_ready, dev_ready = sem("var_ready"), sem("dev_ready")
        z_ready = sem("z_ready")
        ctx_loaded = sem("ctx_loaded")
        z_turned = sem("z_turned")
        zct_ready = sem("zct_ready")
        lay1, act1, lay2, act2, lay3 = sem("lay1"), sem("act1"), sem("lay2"), sem("act2"), sem("lay3")
        y_taken = sem("y_taken")
        y_stored = sem("y_stored")

        block = ctx.enter_context(nc.Block())

        LN_OPS = 8

        @block.sync
        def _(sp):
            def load_ctx(k):
                sp.dma_start(zc[:, :, D:2 * D], ctx_in[k]).then_inc(ctx_loaded, 16)

            def store_y(k):
                sp.wait_ge(y_taken, k + 1)
                sp.dma_start(out[k * CH:(k + 1) * CH, :].rearrange("b o -> o b"), y_sb[:, :]).then_inc(y_stored, 16)

            def stack_block(k, c, first):
                m = c % 2
                sp.wait_ge(parts_ready, k * NC + c + 1)
                if not first or c >= 2:
                    sp.wait_ge(x_stacked[m], k * (NC // 2 * 64) + 64 * (c // 2))
                for r in range(R):
                    sp.dma_start(x_spill[m, :, :, r, :].rearrange("s e b -> e s b"),
                                 parts[E * r:E * r + E, m, :, :]).then_inc(spilled, 16)
                sp.wait_ge(spilled, k * (NC * R * 16) + R * 16 * (c + 1))
                if not first:
                    sp.wait_ge(multiplied, k * NG - NG + LAST_USE[c] + 1)
                elif c == NC // 2:
                    sp.wait_ge(w_spilled, R * 16 * len(W_ROUNDS))
                mid_high = x_spill[m, 0:2].rearrange("s e r b -> (s e) r b")
                high_low = x_spill[m, 1:3].rearrange("s e r b -> (s e) r b")
                for half in range(2):
                    rows_ = slice(64 * half, 64 * half + 64)
                    sp.dma_start(x_a[rows_, c, :, :], mid_high).then_inc(x_stacked[m], 16)
                    sp.dma_start(x_b[rows_, c, :, :], high_low[:, half::2, :]).then_inc(x_stacked[m], 16)

            sp.dma_start(ids_all[:, :, :], ids).then_inc(ids_in, 16)
            sp.dma_start(w_full(0)[:, 0:W_ROUND * P], W_in[:, 0:W_ROUND * P]).then_inc(w_in[0], 16)
            sp.dma_start(w_full(1)[:, 0:W_ROUND * P], W_in[:, W_ROUND * P:2 * W_ROUND * P]).then_inc(w_in[1], 16)
            for dst, src in ((ident, ident_in), (sel, sel_in), (w1, w1_in), (w3, w3_in), (b2, b2_in)):
                sp.dma_start(dst[:, :], src).then_inc(consts_in, 16)
            sp.dma_start(w2[:, :, :], w2_in).then_inc(consts_in, 16)
            sp.dma_start(row_consts[:, :, :], rows_in).then_inc(consts_in, 16)
            sp.dma_start(dw[:, :, :, :], dw_in).then_inc(consts_in, 16)
            load_ctx(0)
            for n, (q0, q1) in enumerate(W_ROUNDS):
                size = (q1 - q0) * P
                sp.wait_ge(w_low, n + 1)
                for r in range(R):
                    sp.dma_start(w_spill[:, :, r, q0 * P:q1 * P].rearrange("s e n -> e s n"),
                                 w_parts(n)[E * r:E * r + E, :, 0:size]).then_inc(w_spilled, 16)
                sp.wait_ge(w_spilled, R * 16 * (n + 1))
                if n + 2 < len(W_ROUNDS):
                    p0, p1 = W_ROUNDS[n + 2]
                    sp.dma_start(w_full(n)[:, 0:(p1 - p0) * P], W_in[:, p0 * P:p1 * P]).then_inc(w_in[n % 2], 16)
                for s, row in ((0, 0), (0, 1), (2, 2), (2, 3)):
                    sp.dma_start(w_a[E * row:E * row + E, :, q0:q1, :].rearrange("e r q n -> e r (q n)"),
                                 w_spill[s, :, :, q0 * P:q1 * P]).then_inc(w_stacked[n], 16)
                for half in range(2):
                    sp.dma_start(w_b[64 * half:64 * half + 64, :, q0:q1, :].rearrange("e r q n -> e r (q n)"),
                                 w_spill[1:3, :, half::2, q0 * P:q1 * P].rearrange("s e r n -> (s e) r n"))\
                      .then_inc(w_stacked[n], 16)

            for c in range(NC):
                stack_block(0, c, True)
            for k in range(1, NCH):
                stack_block(k, 0, False)
                store_y(k - 1)
                sp.wait_ge(y_stored, 16 * k)
                load_ctx(k)
                for c in range(1, NC):
                    stack_block(k, c, False)
            store_y(NCH - 1)
            sp.wait_ge(y_stored, 16 * NCH)

        @block.gpsimd
        def _(pool):
            def gather_chunk(k, first):
                for c in range(NC):
                    if not first or c >= 2:
                        pool.wait_ge(turned, k * NC + c - 1)
                    for r in range(R):
                        for t in range(BT):
                            n = (R * c + r) * BT + t
                            pool.indirect_dma_start(
                                rows[:, c % 2, t, E * r:E * r + E], None, tables[R * c + r],
                                bass.IndirectOffsetOnAxis(ids_all[:, k, n:n + 1], 0))\
                                .then_inc(gathered[c % 2], 16)

            pool.wait_ge(ids_in, 16)
            for k in range(NCH):
                gather_chunk(k, k == 0)
            for m in range(2):
                pool.wait_ge(gathered[m], NCH * (NC // 2) * R * BT * 16)

        @block.scalar
        def _(act):
            def split_block(k, c, first):
                m = c % 2
                act.wait_ge(turned, k * NC + c + 1)
                if not first or c >= 2:
                    last_user = STEP_END[c - 2] if c >= 2 else STEP_END[NC - 2 + c] - NG
                    act.wait_ge(multiplied, k * NG + last_user)
                nc.scalar.activation(xt[:, m, :], turn_ps[:, :], ACT.Copy).then_inc(xt_ready, 1)
                if not first or c >= 2:
                    act.wait_ge(spilled, k * (NC * R * 16) + R * 16 * (c - 1))
                nc.scalar.activation(parts[:, m, 1, :], turn_ps[:, :], ACT.Copy).then_inc(high_ready, 1)
                act.wait_ge(less_high, k * NC + c + 1)
                nc.scalar.activation(parts[:, m, 0, :], turn_ps[:, :], ACT.Copy).then_inc(mid_ready, 1)
                act.wait_ge(less_mid, k * NC + c + 1)
                nc.scalar.activation(parts[:, m, 2, :], turn_ps[:, :], ACT.Copy).then_inc(parts_ready, 1)

            def take_h(k):
                act.wait_ge(summed, k * NBATCH + NBATCH)
                nc.scalar.activation(h_parts[:, :], h_ps[:, :], ACT.Copy).then_inc(h_taken, 1)

            def tower(k):
                act.wait_ge(var_ready, k + 1)
                nc.scalar.activation(stat[:, 1, :], stat[:, 1, :], ACT.Sqrt).then_inc(dev_ready, 1)
                act.wait_ge(z_turned, k + 1)
                nc.scalar.activation(zct[:, :], zct_ps[0:E + 1, :], ACT.Copy).then_inc(zct_ready, 1)
                for n in range(K1):
                    act.wait_ge(lay1, k * K1 + n + 1)
                    nc.scalar.activation(hid1[:, n, :], t_ps[:, 2 + n, :], ACT.Relu).then_inc(act1, 1)
                for n in range(K2):
                    act.wait_ge(lay2, k * K2 + n + 1)
                    nc.scalar.activation(hid2[:, n, :], t_ps[:, n, :], ACT.Relu, bias=b2[:, n:n + 1]).then_inc(act2, 1)
                act.wait_ge(lay3, k + 1)
                act.wait_ge(ctx_loaded, k * 16 + 16)
                nc.scalar.activation(y_sb[:, :], y_ps, ACT.Copy).then_inc(y_taken, 1)

            act.wait_ge(consts_in, 16 * 8)
            nc.scalar.activation(neg_ident[:, :], ident[:, :], ACT.Copy, scale=-1.0).then_inc(neg_made, 1)
            for n, (q0, q1) in enumerate(W_ROUNDS):
                size = (q1 - q0) * P
                act.wait_ge(w_in[n % 2], 16 * (n // 2 + 1))
                if n >= 2:
                    act.wait_ge(w_spilled, R * 16 * (n - 1))
                nc.scalar.activation(w_parts(n)[:, 2, 0:size], w_full(n)[:, 0:size], ACT.Copy).then_inc(w_high, 1)
                act.wait_ge(w_rest, n + 1)
                nc.scalar.activation(w_parts(n)[:, 0, 0:size], w_full(n)[:, 0:size], ACT.Copy).then_inc(w_mid, 1)
            for c in range(NC):
                split_block(0, c, True)
            with act.Fori(1, NCH) as k:
                take_h(k - 1)
                split_block(k, 0, False)
                tower(k - 1)
                for c in range(1, NC):
                    split_block(k, c, False)
            take_h(NCH - 1)
            tower(NCH - 1)

        @block.vector
        def _(dve):
            def multiply_chunk(k, first):
                for g, (c, tiles) in enumerate(GROUPS):
                    if g == STEP_START[c]:
                        dve.wait_ge(xt_ready, k * NC + c + 1)
                    if g == 0 and not first:
                        dve.wait_ge(lay3, k)
                    if g >= Q_SLOTS:
                        dve.wait_ge(summed, k * NBATCH + BATCH_OF[g - Q_SLOTS] + 1)
                    dve.wait_ge(t_ready, k * NG + g + 1)
                    s, n = g % T_SLOTS, len(tiles)
                    x = xt[:, c % 2, :]
                    nc.vector.tensor_tensor(
                        q_buf[:, g % Q_SLOTS, 0:n, :], t_ps[:, GROUP * s:GROUP * s + n, :],
                        x.unsqueeze(1).to_broadcast([P, n, CH]), ALU.mult).then_inc(multiplied, 1)

            def norm(k):
                def step(ins, n):
                    ins.then_inc(ln_step, 1)
                    dve.wait_ge(ln_step, k * LN_OPS + n)

                def wide(ap):
                    return ap.unsqueeze(2).to_broadcast([P, BT, D])

                def const(n):
                    return row_consts[:, n, :].unsqueeze(1).to_broadcast([P, BT, D])

                dve.wait_ge(sum_ready, k + 1)
                step(nc.vector.tensor_tensor(h_sb[:, :, :], sum_ps.rearrange("p (t d) -> p t d", t=BT), const(0),
                                             ALU.add), 1)
                step(nc.vector.tensor_reduce(stat[:, 0, :], h_sb[:, :, :], AX_X, ALU.add), 2)
                step(nc.vector.tensor_scalar(stat[:, 0, :], stat[:, 0, :], 1.0 / D, None, ALU.mult), 3)
                step(nc.vector.tensor_tensor(h_sb[:, :, :], h_sb[:, :, :], wide(stat[:, 0, :]), ALU.subtract), 4)
                step(nc.vector.tensor_tensor(sq[:, :, :], h_sb[:, :, :], h_sb[:, :, :], ALU.mult), 5)
                step(nc.vector.tensor_reduce(stat[:, 1, :], sq[:, :, :], AX_X, ALU.add), 6)
                nc.vector.tensor_scalar(stat[:, 1, :], stat[:, 1, :], 1.0 / D, LN_EPS, ALU.mult, ALU.add)\
                  .then_inc(var_ready, 1)
                dve.wait_ge(dev_ready, k + 1)
                nc.vector.reciprocal(stat[:, 2, :], stat[:, 1, :]).then_inc(ln_step, 1)
                nc.vector.tensor_tensor(sq[:, :, :], h_sb[:, :, :], const(1), ALU.mult).then_inc(ln_step, 1)
                dve.wait_ge(ln_step, k * LN_OPS + LN_OPS)
                nc.vector.tensor_tensor(h_sb[:, :, :], sq[:, :, :], wide(stat[:, 2, :]), ALU.mult).then_inc(z_ready, 1)
                dve.wait_ge(z_ready, 2 * k + 1)
                nc.vector.tensor_tensor(zc[:, :, 0:D], h_sb[:, :, :], const(2), ALU.add).then_inc(z_ready, 1)

            nc.vector.memset(h_ps[:, :], 0.0).then_inc(h_cleared, 1)
            nc.vector.memset(zc[:, :, E:E + 1], 1.0).then_inc(ones_made, 1)
            nc.vector.memset(zc[:, :, E + 1:P], 0.0).then_inc(ones_made, 1)
            for n, (q0, q1) in enumerate(W_ROUNDS):
                size = (q1 - q0) * P
                full = w_full(n)[:, 0:size]
                dve.wait_ge(w_high, n + 1)
                nc.vector.tensor_tensor(full, full, w_parts(n)[:, 2, 0:size], ALU.subtract).then_inc(w_rest, 1)
                dve.wait_ge(w_mid, n + 1)
                nc.vector.tensor_tensor(w_parts(n)[:, 1, 0:size], full, w_parts(n)[:, 0, 0:size],
                                        ALU.subtract).then_inc(w_low, 1)
            dve.wait_ge(consts_in, 16 * 8)
            multiply_chunk(0, True)
            with dve.Fori(1, NCH) as k:
                norm(k - 1)
                multiply_chunk(k, False)
            norm(NCH - 1)

        @block.tensor
        def _(pe):
            mm = nc.tensor.matmul

            def turn(k, c, first):
                pe.wait_ge(gathered[c % 2], k * (NC // 2 * R * BT * 16) + (c // 2 + 1) * R * BT * 16)
                if not first or c >= 1:
                    pe.wait_ge(parts_ready, k * NC + c)
                for t in range(BT):
                    last = mm(turn_ps[:, P * t:P * t + P], rows[:, c % 2, t, :], ident[:, :], is_transpose=True,
                              start=(t == 0), stop=False, skip_group_check=True)
                last.then_inc(turned, 1)

            def take_high(k, c):
                pe.wait_ge(xt_ready, k * NC + c + 1)
                pe.wait_ge(high_ready, k * NC + c + 1)
                mm(turn_ps[:, :], neg_ident[:, :], parts[:, c % 2, 1, :], start=False, stop=False,
                   skip_group_check=True).then_inc(less_high, 1)

            def take_mid(k, c):
                pe.wait_ge(mid_ready, k * NC + c + 1)
                mm(turn_ps[:, :], neg_ident[:, :], parts[:, c % 2, 0, :], start=False, stop=True,
                   skip_group_check=True).then_inc(less_mid, 1)

            def make_tiles(k, g, first):
                c, tiles = GROUPS[g]
                if g >= T_SLOTS:
                    pe.wait_ge(multiplied, k * NG + g - T_SLOTS + 1)
                if g == 0 and not first:
                    pe.wait_ge(y_taken, k)
                for n, (a, r) in enumerate(tiles):
                    if first and r == 0 and a == 0:
                        for w, (q0, q1) in enumerate(W_ROUNDS):
                            if (c == 0 or q0 > pair_slot(c - 1, c - 1)) and q0 <= pair_slot(c, c):
                                pe.wait_ge(w_stacked[w], 6 * 16)
                    if a == c and r == 0:
                        pe.wait_ge(x_stacked[c % 2], k * (NC // 2 * 64) + 64 * (c // 2 + 1))
                    tile = t_ps[:, GROUP * (g % T_SLOTS) + n, :]
                    rows_ = slice(64 * (r % 2), 64 * (r % 2) + 64)
                    q = pair_slot(a, c)
                    mm(tile, w_a[:, r, q, :], x_a[:, a, r, :], start=True, stop=False)
                    last = mm(tile, w_b[rows_, r // 2, q, :], x_b[rows_, a, r // 2, :], start=False, stop=True)
                last.then_inc(t_ready, 1)

            def sum_products(k, b):
                pe.wait_ge(multiplied, k * NG + BATCHES[b][-1] + 1)
                n = 0
                for g in BATCHES[b]:
                    c, tiles = GROUPS[g]
                    for s, (a, r) in enumerate(tiles):
                        final = all(n >= sum(len(GROUPS[x][1]) for x in BATCHES[y]) for y in range(b + 1, NBATCH))
                        last = mm(h_ps[E * n:E * n + D, :], dw[:, r, pair_slot(a, c), :], q_buf[:, g % Q_SLOTS, s, :],
                                  start=(b == 0 or n >= BATCH_MAX[b]), stop=final, skip_group_check=True)
                        n += 1
                last.then_inc(summed, 1)

            BATCH_MAX = [max([sum(len(GROUPS[x][1]) for x in BATCHES[y]) for y in range(b)] or [0]) for b in range(NBATCH)]

            def steps(k, first):
                for g, (c, tiles) in enumerate(GROUPS):
                    make_tiles(k, g, first)
                    if g % 2 == 1 and g >= 3:
                        sum_products(k, (g - 3) // 2)
                    if c < NC - 1:
                        left = STEP_END[c] - 1 - g
                        size = STEP_END[c] - STEP_START[c]
                        if left == min(5, size - 1):
                            turn(k, c + 1, first)
                        if left == min(3, size - 2):
                            take_high(k, c + 1)
                        if left == 0:
                            take_mid(k, c + 1)
                sum_products(k, NBATCH - 1)

            def tower(k, between=()):
                pe.wait_ge(h_taken, k + 1)
                for t in range(BT):
                    last = mm(sum_ps[:, D * t:D * t + D], h_parts[:, P * t:P * t + P], sel[:, :],
                              start=(t == 0), stop=(t == BT - 1), skip_group_check=True)
                last.then_inc(sum_ready, 1)
                for work in between:
                    work()
                pe.wait_ge(z_ready, 2 * k + 2)
                pe.wait_ge(ctx_loaded, k * 16 + 16)
                for t in range(BT):
                    last = mm(zct_ps[:, P * t:P * t + P], zc[:, t, :], ident[:, :], is_transpose=True,
                              start=(t == 0), stop=(t == BT - 1), skip_group_check=True)
                last.then_inc(z_turned, 1)
                pe.wait_ge(zct_ready, k + 1)
                for n in range(K1):
                    mm(t_ps[:, 2 + n, :], w1[:, P * n:P * n + P], zct[:, :], start=True, stop=True).then_inc(lay1, 1)
                for n in range(K2):
                    for m in range(K1):
                        if n == 0:
                            pe.wait_ge(act1, k * K1 + m + 1)
                        last = mm(t_ps[:, n, :], w2[:, m, P * n:P * n + P], hid1[:, m, :],
                                  start=(m == 0), stop=(m == K1 - 1))
                    last.then_inc(lay2, 1)
                for m in range(K2):
                    pe.wait_ge(act2, k * K2 + m + 1)
                    last = mm(y_ps, w3[:, m:m + 1], hid2[:, m, :], start=(m == 0), stop=(m == K2 - 1))
                last.then_inc(lay3, 1)

            pe.wait_ge(consts_in, 16 * 8)
            pe.wait_ge(neg_made, 1)
            pe.wait_ge(ones_made, 2)
            pe.wait_ge(h_cleared, 1)
            turn(0, 0, True)
            take_high(0, 0)
            take_mid(0, 0)
            steps(0, True)
            with pe.Fori(1, NCH) as k:
                turn(k, 0, False)
                tower(k - 1, between=(lambda: take_high(k, 0), lambda: take_mid(k, 0)))
                steps(k, False)
            tower(NCH - 1)


def kernel(**inputs):
    import numpy as np
    import concourse.bacc as bacc
    from concourse import mybir as mb
    from concourse.bass_utils import run_bass_kernel_spmd as run

    a = {n: np.ascontiguousarray(v) for n, v in inputs.items()}
    ids = a["ids"].reshape(NCH, BT, P, FIELDS).transpose(2, 0, 3, 1).reshape(P, NCH, FIELDS * BT)
    W, dense_w = a["L0_rec_W"], a["L0_rec_dense_w"]
    w_tiles = np.zeros((R, E, NQ, R, E), W.dtype)
    dw_tiles = np.zeros((R, E, R, NQ, D), dense_w.dtype)
    pair = 0
    for i in range(FIELDS):
        for j in range(i + 1, FIELDS):
            q = pair_slot(i // R, j // R)
            w_tiles[i % R, :, q, j % R, :] = W[pair]
            dw_tiles[j % R, :, i % R, q, :] = dense_w[pair]
            pair += 1
    sel = np.zeros((P, D), np.float32)
    for g in range(R):
        sel[E * g:E * g + D] = np.eye(D, dtype=np.float32)
    rows = np.stack([a["L0_rec_dense_b"], a["L0_rec_gamma"], a["L0_rec_beta"]])
    arrays = {
        "ids": ids,
        "dense_ctx": a["dense_ctx"].reshape(NCH, BT, P, D).transpose(0, 2, 1, 3),
        "W": w_tiles.reshape(P, NQ * P),
        "dense_w": dw_tiles.reshape(P, R, NQ, D),
        "w1": np.concatenate([a["W_top1"], a["b_top1"][None]]),
        "w2": a["W_top2"].reshape(K1, P, H2).transpose(1, 0, 2),
        "w3": a["W_top3"].reshape(K2, P).T,
        "b2": a["b_top2"].reshape(K2, P).T,
        "rows": np.broadcast_to(rows[None], (P, 3, D)),
        "ident": np.eye(P, dtype=np.float32),
        "sel": sel,
    }
    for f in range(FIELDS):
        arrays[f"tbl_{f}"] = a[f"tbl_{f}"]
    arrays = {f"in_{n}": np.ascontiguousarray(v) for n, v in arrays.items()}

    nc = bacc.Bacc("TRN2", target_bir_lowering=False, num_devices=1)
    args = [nc.dram_tensor(n, v.shape, mb.dt.from_np(v.dtype), kind="ExternalInput").ap() for n, v in arrays.items()]
    out = nc.dram_tensor("out_y", (BATCH, 1), F32, kind="ExternalOutput").ap()
    build(nc, *args, out)
    r = run(nc, [arrays], core_ids=[0])
    return r.results[0]["out_y"]
```

```python
from contextlib import ExitStack

import concourse.bass as bass
from concourse import mybir

F32 = mybir.dt.float32
F32R = mybir.dt.float32r
F16 = mybir.dt.float16
BF16 = mybir.dt.bfloat16
I32 = mybir.dt.int32
ALU = mybir.AluOpType
ACT = mybir.ActivationFunctionType
AX_X = mybir.AxisListType.X

P = 128
BATCH = 2048
FIELDS = 40
E = 32
D = 16
CH = 256
NCH = BATCH // CH
BT = CH // P
R = P // E
NC = FIELDS // R
H1, H2 = 512, 256
K1 = H1 // P
K2 = H2 // P
LN_EPS = 1e-3

GROUPS = [(c, a, R if a < c else R - 1) for c in range(NC) for a in range(c + 1)]
NG = len(GROUPS)
TILE0 = [sum(n for _, _, n in GROUPS[:g]) for g in range(NG + 1)]
NT = TILE0[-1]
STEP_START = [c * (c + 1) // 2 for c in range(NC + 1)]

LOOKED = 2
SMALL = (5, 10, 11, 14, 20, 21, 23, 29)
ORDER = SMALL + tuple(f for f in range(FIELDS) if f not in SMALL)
TABLE = 1000
KT = 8
KP = TABLE // KT
HT = KT // 2
FETCHED = NC - LOOKED

T_SLOTS = 3
Q_SLOTS = 3
XT_SLOT = [0, 1, 2, 3, 0, 1, 2, 0, 1, 3]
XT_SLOTS = max(XT_SLOT) + 1
ROW_SLOTS = 4
LAG = 2

W_PIECES = [(0, 3), (3, 5), (5, 6), (6, 7), (7, 8), (8, 9), (9, 10)]
W_TILES = [(TILE0[STEP_START[c0]], TILE0[STEP_START[c1]]) for c0, c1 in W_PIECES]

LOOK_AT = {33 + t: (0, t) for t in range(KT)} | {42 + t: (1, t) for t in range(KT)}
MASK_AT = {g - 1: at for g, at in LOOK_AT.items()}
TURN_AT = {40: 0, 49: 1, 51: 2, 0: 3, 3: 4, 9: 5, 15: 6, 21: 7, 28: 8, 31: 9}
HIGH_AT = {g + 1: c for g, c in TURN_AT.items()}
AHEAD = 3
TOWER_AT = {5: "sum", 17: "turn", 18: 0, 19: 1, 20: 2, 23: 3, 24: "wide0", 26: "wide1", 27: "last"}
NORM_AT = 7


def build(nc, ids, small_ids, iota_in, ctx_in, W_in, dw_in, w1_in, w2_in, w3_in, b2_in, rows_in, ident_in, sel_in, *rest):
    tables, out = rest[:FIELDS], rest[FIELDS]

    with ExitStack() as ctx:
        def sb(name, shape, dt):
            return ctx.enter_context(nc.sbuf_tensor(name, shape, dt))

        def sem(name):
            return ctx.enter_context(nc.semaphore(name))

        w_a = sb("w_a", [P, NT * P], F32R)
        x_a = sb("x_a", [P, NC, R, CH], F32R)
        dw = sb("dw", [P, NT, D], F32)
        q_buf = sb("q_buf", [P, Q_SLOTS, R, CH], F32)
        xt = sb("xt", [P, XT_SLOTS, CH], F32)
        rows = sb("rows", [P, ROW_SLOTS, BT, P], F32)
        parts = sb("parts", [P, 2, 2, CH], F32R)
        ids_all = sb("ids_all", [P, NCH, FETCHED * R * BT], I32)
        look_w = sb("look_w", [P, KT, 3, P], BF16)
        iota = sb("iota", [P, KT], F32)
        ident = sb("ident", [P, P], F32)
        neg_ident = sb("neg_ident", [P, P], F32R)
        sel = sb("sel", [P, D], F32)
        w1 = sb("w1", [E + 1, H1], F32)
        w2 = sb("w2", [P, K1, H2], F32)
        w3 = sb("w3", [P, K2], F32)
        b2 = sb("b2", [P, K2], F32)
        row_consts = sb("row_consts", [P, 3, D], F32)
        h_sb = sb("h_sb", [P, BT, D], F32)
        sq = sb("sq", [P, BT, D], F32)
        stat = sb("stat", [P, 3, BT], F32)
        zc = sb("zc", [P, BT, P], F32)
        zct = sb("zct", [E + 1, CH], F32)
        hid1 = sb("hid1", [P, K1, CH], F32)
        hid2 = sb("hid2", [P, K2, CH], F32)
        h_parts = hid2[:, 0, :]
        y_sb = zct[0:1, :]
        masks = hid1[:, :, :].rearrange("p k b -> p (k b)").bitcast(BF16).rearrange("p (s c) -> p s c", s=2)
        ids16 = hid2[:, :, :].rearrange("p k b -> p (k b)").bitcast(F16)
        raw_tables = [x[:, :, :].rearrange("p k b -> p (k b)") for x in (hid1, w2)]
        raw_ids = xt[0:NCH * LOOKED * R, 0, :].bitcast(I32)
        part_ids = xt[0:NCH * LOOKED * R, 1, 0:CH // 2].bitcast(F16)
        flat_q = q_buf[:, :, :, :].rearrange("p g r b -> p (g r b)")
        flat_dw = dw[:, :, :].rearrange("p t d -> p (t d)")
        w_raw = []
        for n, (t0, t1) in enumerate(W_TILES):
            room, start = (flat_dw, W_TILES[3][0]) if 3 <= n < 6 else (flat_q, t0 if n == 6 else 0)
            w_raw.append(room[:, (t0 - start) * E:(t1 - start) * E])
        w_stage = w_a[:, NT * P // 2:].rearrange("p (s c) -> p s c", s=2)

        t_ps = ctx.enter_context(nc.psum_tensor("t_ps", [P, T_SLOTS, R, CH], F32))
        side_ps = ctx.enter_context(nc.psum_tensor("side_ps", [P, 2, CH], F32))
        h_ps = ctx.enter_context(nc.psum_tensor("h_ps", [P, CH], F32))
        turn_ps = side_ps[:, 0, :]
        tower_ps = side_ps[:, 1, :]

        w_parts = [nc.dram_tensor(f"w_parts{n}", [2, P, (t1 - t0) * E], F32, kind="Internal").ap()
                   for n, (t0, t1) in enumerate(W_TILES)]
        tables_split = nc.dram_tensor("tables_split", [LOOKED, P, KT * 3 * P], BF16, kind="Internal").ap()
        ids_small = nc.dram_tensor("ids_small", [NCH * LOOKED, R * CH], F16, kind="Internal").ap()
        x_spill = nc.dram_tensor("x_spill", [2, 2, E, R, CH], F32, kind="Internal").ap()

        ids_in = sem("ids_in")
        consts_in = sem("consts_in")
        ident_loaded, dw_loaded = sem("ident_loaded"), sem("dw_loaded")
        raw_in = [sem(f"raw_in{n}") for n in range(len(W_PIECES))]
        w_high_ready, w_split = sem("w_high_ready"), sem("w_split")
        w_written = [sem(f"w_written{n}") for n in range(len(W_PIECES))]
        w_in = [sem(f"w_in{n}") for n in range(len(W_PIECES))]
        neg_made, zc_filled, h_cleared, look_cleared = (sem("neg_made"), sem("zc_filled"), sem("h_cleared"),
                                                        sem("look_cleared"))
        tables_in = [sem(f"tables_in{n}") for n in range(LOOKED)]
        tables_high, tables_rest, tables_mid = sem("tables_high"), sem("tables_rest"), sem("tables_mid")
        tables_low = sem("tables_low")
        tables_out = [sem(f"tables_out{n}") for n in range(LOOKED)]
        iota_loaded, small_in, small_ready, small_out = (sem("iota_loaded"), sem("small_in"), sem("small_ready"),
                                                         sem("small_out"))
        ids16_loaded, mask_ready, looked_up = sem("ids16_loaded"), sem("mask_ready"), sem("looked_up")
        half_loaded = [sem(f"half_loaded{n}") for n in range(2)]
        gathered = [sem(f"gathered{n}") for n in range(ROW_SLOTS)]
        turned, xt_ready, high_ready = sem("turned"), sem("xt_ready"), sem("high_ready")
        less_high, parts_ready = sem("less_high"), sem("parts_ready")
        spilled = [sem(f"spilled{n}") for n in range(2)]
        x_stacked = [sem(f"x_stacked{n}") for n in range(2)]
        t_ready, multiplied, summed = sem("t_ready"), sem("multiplied"), sem("summed")
        h_taken, sum_ready = sem("h_taken"), sem("sum_ready")
        ln_step, var_ready, dev_ready, z_ready = sem("ln_step"), sem("var_ready"), sem("dev_ready"), sem("z_ready")
        ctx_loaded, z_turned, zct_ready = sem("ctx_loaded"), sem("z_turned"), sem("zct_ready")
        lay1, act1, lay2, act2, lay3 = sem("lay1"), sem("act1"), sem("lay2"), sem("act2"), sem("lay3")
        y_taken, y_stored = sem("y_taken"), sem("y_stored")

        block = ctx.enter_context(nc.Block())

        NORM_STEPS = 8
        PER_SLOT = FETCHED // ROW_SLOTS * R * BT * 16

        def by_part(c):
            return raw_tables[c][0:KP, :].rearrange("p (r t e) -> p r t e", r=R, t=KT)

        def split_tables(s):
            return look_w[0:KP, :, s, :].rearrange("p t (r e) -> p r t e", r=R)

        @block.sync
        def _(sp):
            def load_ctx(k):
                sp.dma_start(zc[:, :, D:2 * D], ctx_in[k]).then_inc(ctx_loaded, 16)

            def store_y(k):
                sp.wait_ge(y_taken, k + 1)
                sp.dma_start(out[k * CH:(k + 1) * CH, :].rearrange("b o -> o b"), y_sb).then_inc(y_stored, 16)

            def send_block(k, c):
                m, n = c % 2, k * NC + c
                sp.wait_ge(parts_ready, n + 1)
                if n >= 2:
                    sp.wait_ge(x_stacked[m], 32 * (n // 2))
                for r in range(R):
                    sp.dma_start(x_spill[m, :, :, r, :].rearrange("s e b -> e s b"),
                                 parts[E * r:E * r + E, m, :, :].bitcast(F32)).then_inc(spilled[m], 16)

            def stack_block(k, c):
                m, n = c % 2, k * NC + c
                sp.wait_ge(spilled[m], R * 16 * (n // 2 + 1))
                if k:
                    last_use = STEP_START[NC - 1] + c
                    sp.wait_ge(multiplied, (k - 1) * NG + last_use + 1)
                for half in range(2):
                    sp.dma_start(x_a[64 * half:64 * half + 64, c, :, :].bitcast(F32),
                                 x_spill[m].rearrange("s e r b -> (s e) r b")).then_inc(x_stacked[m], 16)

            def load_ids16(k, c):
                n = k * LOOKED + c
                if n:
                    sp.wait_ge(mask_ready, n * KT)
                if k > 1:
                    sp.wait_ge(lay3, k - 1)
                sp.dma_start(ids16, ids_small[n:n + 1, :].to_broadcast([P, R * CH])).then_inc(ids16_loaded, 16)

            def load_half(k, c, h):
                n = k * LOOKED + c
                if n == 1:
                    sp.wait_ge(tables_out[0], 16)
                sp.wait_ge(looked_up, (n - 1) * KT + HT * (h + 1))
                sp.dma_start(look_w[:, HT * h:HT * h + HT, :, :],
                             tables_split[c, :, HT * 3 * P * h:HT * 3 * P * (h + 1)]
                             .rearrange("p (t s c) -> p t s c", t=HT, s=3)).then_inc(half_loaded[h], 16)

            sp.dma_start(ids_all[:, :, :], ids).then_inc(ids_in, 16)
            sp.dma_start(raw_ids, small_ids).then_inc(small_in, 16)
            for c in reversed(range(LOOKED)):
                for r in range(R):
                    sp.dma_start(raw_tables[c][0:KP, r * KT * E:(r + 1) * KT * E],
                                 tables[ORDER[R * c + r]].rearrange("(p t) e -> p (t e)", t=KT))\
                      .then_inc(tables_in[c], 16)
            sp.dma_start(iota[:, :], iota_in).then_inc(iota_loaded, 16)
            sp.dma_start(ident[:, :], ident_in).then_inc(ident_loaded, 16)
            def load_raw(n):
                t0, t1 = W_TILES[n]
                sp.dma_start(w_raw[n], W_in[:, t0 * E:t1 * E]).then_inc(raw_in[n], 16)

            def keep_tables(c):
                sp.wait_ge(tables_low, LOOKED - c)
                sp.dma_start(tables_split[c], look_w[:, :, :, :].rearrange("p t s c -> p (t s c)"))\
                  .then_inc(tables_out[c], 16)

            def keep_w(n):
                t0, t1 = W_TILES[n]
                sp.wait_ge(w_split, n + 1)
                sp.dma_start(w_parts[n].rearrange("s p c -> p s c"),
                             w_stage[:, :, t0 * E:t1 * E].bitcast(F32)).then_inc(w_written[n], 16)

            def load_w(n):
                t0, t1 = W_TILES[n]
                sp.wait_ge(w_written[n], 16)
                if t1 > NT // 2:
                    for m in range(n, len(W_PIECES)):
                        sp.wait_ge(w_written[m], 16)
                for g in range(R):
                    sp.dma_start(w_a[E * g:E * g + E, t0 * P:t1 * P].bitcast(F32),
                                 w_parts[n][g // 2].rearrange("(e q) c -> e (q c)", q=P // E)).then_inc(w_in[n], 16)

            for n in range(6):
                load_raw(n)
            sp.wait_ge(small_ready, 1)
            sp.dma_start(ids_small.rearrange("n (r b) -> (n r) b", r=R), part_ids).then_inc(small_out, 16)
            keep_tables(1)
            sp.wait_ge(small_out, 16)
            load_ids16(0, 0)
            for n in range(3):
                keep_w(n)
            load_raw(6)
            keep_tables(0)
            load_w(0)
            load_half(0, 1, 0)
            load_ids16(0, 1)
            load_half(0, 1, 1)
            send_block(0, 0)
            keep_w(3)
            stack_block(0, 0)
            keep_w(4)
            keep_w(5)
            sp.dma_start(dw[:, :, :], dw_in).then_inc(dw_loaded, 16)
            send_block(0, 1)
            load_w(1)
            send_block(0, 2)
            stack_block(0, 1)
            keep_w(6)
            stack_block(0, 2)
            load_w(2)
            for dst, src in ((sel, sel_in), (w1, w1_in), (w3, w3_in), (b2, b2_in)):
                sp.dma_start(dst[:, :], src).then_inc(consts_in, 16)
            for dst, src in ((w2, w2_in), (row_consts, rows_in)):
                sp.dma_start(dst[:, :, :], src).then_inc(consts_in, 16)
            load_ctx(0)
            W_LOAD_AT = {3: [3], 4: [4], 6: [5], 7: [6]}
            for k in range(NCH):
                for c in range(NC):
                    if c == 8 and k + 1 < NCH:
                        load_ids16(k + 1, 0)
                    if c == 8 and k:
                        store_y(k - 1)
                    if k == 0 and c in W_LOAD_AT:
                        for n in W_LOAD_AT[c]:
                            load_w(n)
                    if c >= AHEAD:
                        send_block(k, c)
                        stack_block(k, c)
                    if c == 5 and k + 1 < NCH:
                        load_half(k + 1, 0, 0)
                        load_half(k + 1, 0, 1)
                if k:
                    sp.wait_ge(y_stored, 16 * k)
                    load_ctx(k)
                if k + 1 < NCH:
                    load_half(k + 1, 1, 0)
                    load_ids16(k + 1, 1)
                    load_half(k + 1, 1, 1)
                    send_block(k + 1, 0)
                    stack_block(k + 1, 0)
                    send_block(k + 1, 1)
                    send_block(k + 1, 2)
                    stack_block(k + 1, 1)
                    stack_block(k + 1, 2)
            store_y(NCH - 1)
            sp.wait_ge(y_stored, 16 * NCH)

        @block.gpsimd
        def _(pool):
            pool.wait_ge(ids_in, 16)
            for k in range(NCH):
                for j in range(FETCHED):
                    n = k * FETCHED + j
                    if n >= ROW_SLOTS:
                        pool.wait_ge(turned, n - ROW_SLOTS + 1)
                    for r in range(R):
                        for t in range(BT):
                            i = (R * j + r) * BT + t
                            pool.indirect_dma_start(
                                rows[:, j % ROW_SLOTS, t, E * r:E * r + E], None, tables[ORDER[R * (j + LOOKED) + r]],
                                bass.IndirectOffsetOnAxis(ids_all[:, k, i:i + 1], 0))\
                                .then_inc(gathered[j % ROW_SLOTS], 16)
            for m in range(ROW_SLOTS):
                pool.wait_ge(gathered[m], NCH * PER_SLOT)

        @block.scalar
        def _(act):
            copy = ACT.Copy

            def first_parts(k, c, first):
                if c < LOOKED:
                    act.wait_ge(looked_up, (k * LOOKED + c + 1) * KT)
                else:
                    act.wait_ge(turned, k * FETCHED + c - LOOKED + 1)
                before = [x for x in range(c) if XT_SLOT[x] == XT_SLOT[c]]
                if before:
                    act.wait_ge(multiplied, k * NG + STEP_START[before[-1] + 1])
                elif not first:
                    step = max(x for x in range(NC) if XT_SLOT[x] == XT_SLOT[c])
                    act.wait_ge(multiplied, k * NG - NG + STEP_START[step + 1])
                nc.scalar.activation(xt[:, XT_SLOT[c], :], turn_ps, copy).then_inc(xt_ready, 1)
                if not first or c >= 2:
                    act.wait_ge(spilled[c % 2], k * (NC // 2 * R * 16) + R * 16 * (c // 2))
                nc.scalar.activation(parts[:, c % 2, 0, :], turn_ps, copy).then_inc(high_ready, 1)

            def low_part(k, c):
                act.wait_ge(less_high, k * NC + c + 1)
                nc.scalar.activation(parts[:, c % 2, 1, :], turn_ps, copy).then_inc(parts_ready, 1)

            def split_w(n):
                t0, t1 = W_TILES[n]
                act.wait_ge(raw_in[n], 16)
                nc.scalar.activation(w_stage[:, 0, t0 * E:t1 * E], w_raw[n], copy)\
                  .then_inc(w_high_ready, 1)

            def take_h(k):
                act.wait_ge(summed, k * NG + NG)
                nc.scalar.activation(h_parts, h_ps[:, :], copy).then_inc(h_taken, 1)

            def tower(k, piece):
                if piece == "turn":
                    act.wait_ge(z_turned, k + 1)
                    act.wait_ge(ctx_loaded, k * 16 + 16)
                    nc.scalar.activation(zct[:, :], tower_ps[0:E + 1, :], copy).then_inc(zct_ready, 1)
                elif piece == "last":
                    act.wait_ge(lay3, k + 1)
                    nc.scalar.activation(y_sb, tower_ps[0:1, :], copy).then_inc(y_taken, 1)
                elif piece in ("wide0", "wide1"):
                    n = int(piece[-1])
                    act.wait_ge(lay2, k * K2 + n + 1)
                    nc.scalar.activation(hid2[:, n, :], tower_ps, ACT.Relu, bias=b2[:, n:n + 1]).then_inc(act2, 1)
                elif piece != "sum":
                    act.wait_ge(lay1, k * K1 + piece + 1)
                    nc.scalar.activation(hid1[:, piece, :], tower_ps, ACT.Relu).then_inc(act1, 1)

            def root(k):
                act.wait_ge(var_ready, k + 1)
                nc.scalar.activation(stat[:, 1, :], stat[:, 1, :], ACT.Sqrt).then_inc(dev_ready, 1)

            def chunk(k, first, last):
                for g in range(NG):
                    if g == LAG - 1 and not first:
                        take_h(k - 1)
                    if g in HIGH_AT and (HIGH_AT[g] >= AHEAD or not last):
                        c = HIGH_AT[g]
                        low_part(k if c >= AHEAD else k + 1, c)
                    if g in TOWER_AT and not first:
                        tower(k - 1, TOWER_AT[g])
                    if g == NORM_AT + 7 and not first:
                        root(k - 1)
                    if g in TURN_AT and (TURN_AT[g] >= AHEAD or not last):
                        c = TURN_AT[g]
                        first_parts(k if c >= AHEAD else k + 1, c, first and c >= AHEAD)

            act.wait_ge(ident_loaded, 16)
            nc.scalar.activation(neg_ident[:, :], ident[:, :], copy, scale=-1.0).then_inc(neg_made, 1)
            act.wait_ge(small_in, 16)
            nc.scalar.activation(part_ids, raw_ids, copy).then_inc(small_ready, 1)
            for n, c in enumerate(reversed(range(LOOKED))):
                act.wait_ge(tables_in[c], R * 16)
                if n:
                    act.wait_ge(tables_out[c + 1], 16)
                else:
                    act.wait_ge(look_cleared, 1)
                nc.scalar.activation(split_tables(0), by_part(c), copy).then_inc(tables_high, 1)
                act.wait_ge(tables_rest, n + 1)
                nc.scalar.activation(split_tables(1), by_part(c), copy).then_inc(tables_mid, 1)
                for piece in range(3 * n, 3 * n + 3 if n == 0 else len(W_PIECES)):
                    split_w(piece)
            for c in range(AHEAD):
                first_parts(0, c, True)
                low_part(0, c)
            chunk(0, True, False)
            act.wait_ge(consts_in, 16 * 6)
            with act.Fori(1, NCH - 1) as k:
                chunk(k, False, False)
            chunk(NCH - 1, False, True)
            take_h(NCH - 1)
            root(NCH - 1)
            for piece in TOWER_AT.values():
                tower(NCH - 1, piece)

        @block.vector
        def _(dve):
            def split_w(n):
                t0, t1 = W_TILES[n]
                dve.wait_ge(w_high_ready, n + 1)
                nc.vector.tensor_tensor(w_stage[:, 1, t0 * E:t1 * E], w_raw[n],
                                        w_stage[:, 0, t0 * E:t1 * E].bitcast(F32), ALU.subtract)\
                  .then_inc(w_split, 1)

            def multiply(k, g, first):
                c, _, n = GROUPS[g]
                if g == STEP_START[c]:
                    dve.wait_ge(xt_ready, k * NC + c + 1)
                if g >= Q_SLOTS:
                    dve.wait_ge(summed, k * NG + g - Q_SLOTS + 1)
                elif not first:
                    before = max(x for x in range(NG) if x % Q_SLOTS == g)
                    dve.wait_ge(summed, k * NG - NG + before + 1)
                dve.wait_ge(t_ready, k * NG + g + 1)
                x = xt[:, XT_SLOT[c], :].unsqueeze(1).to_broadcast([P, n, CH])
                nc.vector.tensor_tensor(q_buf[:, g % Q_SLOTS, 0:n, :], t_ps[:, g % T_SLOTS, 0:n, :], x,
                                        ALU.mult).then_inc(multiplied, 1)

            def wide(ap):
                return ap.unsqueeze(2).to_broadcast([P, BT, D])

            def const(n):
                return row_consts[:, n, :].unsqueeze(1).to_broadcast([P, BT, D])

            def norm(k, n):
                def after(count):
                    dve.wait_ge(ln_step, k * NORM_STEPS + count)

                v = nc.vector
                total, var, inv = stat[:, 0, :], stat[:, 1, :], stat[:, 2, :]
                if n == 0:
                    dve.wait_ge(sum_ready, k + 1)
                    h = tower_ps[:, 0:BT * D].rearrange("p (t d) -> p t d", t=BT)
                    v.tensor_tensor(h_sb[:, :, :], h, const(0), ALU.add).then_inc(ln_step, 1)
                elif n == 1:
                    after(1)
                    v.tensor_reduce(total, h_sb[:, :, :], AX_X, ALU.add).then_inc(ln_step, 1)
                elif n == 2:
                    after(2)
                    v.tensor_scalar(total, total, 1.0 / D, None, ALU.mult).then_inc(ln_step, 1)
                elif n == 3:
                    after(3)
                    v.tensor_tensor(h_sb[:, :, :], h_sb[:, :, :], wide(total), ALU.subtract).then_inc(ln_step, 1)
                elif n == 4:
                    after(4)
                    v.tensor_tensor(sq[:, :, :], h_sb[:, :, :], h_sb[:, :, :], ALU.mult).then_inc(ln_step, 1)
                elif n == 5:
                    after(5)
                    v.tensor_reduce(var, sq[:, :, :], AX_X, ALU.add).then_inc(ln_step, 1)
                elif n == 6:
                    after(6)
                    v.tensor_scalar(var, var, 1.0 / D, LN_EPS, ALU.mult, ALU.add).then_inc(var_ready, 1)
                elif n == 7:
                    v.tensor_tensor(sq[:, :, :], h_sb[:, :, :], const(1), ALU.mult).then_inc(ln_step, 1)
                    dve.wait_ge(dev_ready, k + 1)
                    v.reciprocal(inv, var).then_inc(ln_step, 1)
                elif n == 8:
                    after(NORM_STEPS)
                    v.tensor_tensor(h_sb[:, :, :], sq[:, :, :], wide(inv), ALU.mult).then_inc(z_ready, 1)
                elif n == 9:
                    dve.wait_ge(z_ready, 2 * k + 1)
                    v.tensor_tensor(zc[:, :, 0:D], h_sb[:, :, :], const(2), ALU.add).then_inc(z_ready, 1)

            def make_mask(k, c, t):
                n = (k * LOOKED + c) * KT + t
                if t == 0:
                    dve.wait_ge(ids16_loaded, (k * LOOKED + c) * 16 + 16)
                if not isinstance(n, int) or n >= 2:
                    dve.wait_ge(looked_up, n - 1)
                nc.vector.tensor_scalar(masks[0:KP, t % 2, :], ids16[0:KP, :], iota[0:KP, t:t + 1], None,
                                        ALU.is_equal).then_inc(mask_ready, 1)

            def chunk(k, first, last):
                for g in range(NG):
                    multiply(k, g, first)
                    if NORM_AT <= g < NORM_AT + 10 and not first:
                        norm(k - 1, g - NORM_AT)
                    if g in MASK_AT and not last:
                        make_mask(k + 1, *MASK_AT[g])

            nc.vector.memset(look_w[:, :, :, :], 0.0).then_inc(look_cleared, 1)
            nc.vector.memset(h_ps[:, :], 0.0).then_inc(h_cleared, 1)
            nc.vector.memset(zc[:, :, E:E + 1], 1.0).then_inc(zc_filled, 1)
            nc.vector.memset(zc[:, :, E + 1:P], 0.0).then_inc(zc_filled, 1)
            for n, c in enumerate(reversed(range(LOOKED))):
                dve.wait_ge(tables_high, n + 1)
                nc.vector.tensor_tensor(by_part(c), by_part(c), split_tables(0), ALU.subtract).then_inc(tables_rest, 1)
                dve.wait_ge(tables_mid, n + 1)
                nc.vector.tensor_tensor(split_tables(2), by_part(c), split_tables(1), ALU.subtract)\
                  .then_inc(tables_low, 1)
                if n == 0:
                    for piece in range(3):
                        split_w(piece)
            dve.wait_ge(iota_loaded, 16)
            dve.wait_ge(tables_low, LOOKED)
            for t in range(KT):
                make_mask(0, 0, t)
                if t % 2:
                    split_w(3 + t // 2)
            for t in range(KT):
                make_mask(0, 1, t)
            chunk(0, True, False)
            dve.wait_ge(consts_in, 16 * 6)
            with dve.Fori(1, NCH - 1) as k:
                chunk(k, False, False)
            chunk(NCH - 1, False, True)
            for n in range(10):
                norm(NCH - 1, n)

        @block.tensor
        def _(pe):
            mm = nc.tensor.matmul

            def turn(k, c, first):
                j = c - LOOKED
                pe.wait_ge(gathered[j % ROW_SLOTS], k * PER_SLOT + (j // ROW_SLOTS + 1) * R * BT * 16)
                if not first or c >= 1:
                    pe.wait_ge(parts_ready, k * NC + c)
                for t in range(BT):
                    last = mm(turn_ps[:, P * t:P * t + P], rows[:, j % ROW_SLOTS, t, :], ident[:, :],
                              is_transpose=True, start=(t == 0), stop=False, skip_group_check=True)
                last.then_inc(turned, 1)

            def look_up(k, c, t, first):
                if t == 0 and not (first and c == 0):
                    pe.wait_ge(parts_ready, k * NC + c)
                if first and c == 0:
                    pe.wait_ge(tables_low, LOOKED)
                elif t % HT == 0:
                    pe.wait_ge(half_loaded[t // HT], (k * LOOKED + c) * 16)
                pe.wait_ge(mask_ready, (k * LOOKED + c) * KT + t + 1)
                for s in range(3):
                    for r in range(R):
                        last = mm(turn_ps[E * r:E * r + E, :], look_w[0:KP, t, s, E * r:E * r + E],
                                  masks[0:KP, t % 2, CH * r:CH * r + CH], start=(t == 0 and s == 0), stop=False,
                                  skip_group_check=True)
                last.then_inc(looked_up, 1)

            def take_high(k, c):
                pe.wait_ge(xt_ready, k * NC + c + 1)
                pe.wait_ge(high_ready, k * NC + c + 1)
                mm(turn_ps, neg_ident[:, :], parts[:, c % 2, 0, :], start=False, stop=True,
                   skip_group_check=True).then_inc(less_high, 1)

            def make_tiles(k, g, first):
                c, a, n = GROUPS[g]
                if g >= T_SLOTS:
                    pe.wait_ge(multiplied, k * NG + g - T_SLOTS + 1)
                elif not first:
                    before = max(x for x in range(NG) if x % T_SLOTS == g)
                    pe.wait_ge(multiplied, k * NG - NG + before + 1)
                if first and a == 0:
                    for piece, (c0, _) in enumerate(W_PIECES):
                        if c0 == c:
                            pe.wait_ge(w_in[piece], R * 16)
                if a == c:
                    pe.wait_ge(x_stacked[c % 2], k * (NC // 2 * 32) + 32 * (c // 2 + 1))
                for r in range(n):
                    tile = TILE0[g] + r
                    last = mm(t_ps[:, g % T_SLOTS, r, :], w_a[:, tile * P:tile * P + P], x_a[:, a, r, :],
                              start=True, stop=True)
                last.then_inc(t_ready, 1)

            def sum_products(k, g):
                pe.wait_ge(multiplied, k * NG + g + 1)
                for r in range(GROUPS[g][2]):
                    last = mm(h_ps[E * r:E * r + D, :], dw[:, TILE0[g] + r, :], q_buf[:, g % Q_SLOTS, r, :],
                              start=(g == 0 or (g == 1 and r == R - 1)), stop=(g >= NG - 2),
                              skip_group_check=True)
                last.then_inc(summed, 1)

            def tower(k, piece):
                if piece == "sum":
                    for t in range(BT):
                        last = mm(tower_ps[:, D * t:D * t + D], h_parts[:, P * t:P * t + P], sel[:, :],
                                  start=(t == 0), stop=(t == BT - 1), skip_group_check=True)
                    last.then_inc(sum_ready, 1)
                elif piece == "turn":
                    pe.wait_ge(z_ready, 2 * k + 2)
                    pe.wait_ge(ctx_loaded, k * 16 + 16)
                    for t in range(BT):
                        last = mm(tower_ps[:, P * t:P * t + P], zc[:, t, :], ident[:, :], is_transpose=True,
                                  start=(t == 0), stop=(t == BT - 1), skip_group_check=True)
                    last.then_inc(z_turned, 1)
                elif piece in ("wide0", "wide1"):
                    n = int(piece[-1])
                    if n == 0:
                        pe.wait_ge(act1, k * K1 + K1)
                    else:
                        pe.wait_ge(act2, k * K2 + n)
                    for m in range(K1):
                        last = mm(tower_ps, w2[:, m, P * n:P * n + P], hid1[:, m, :], start=(m == 0),
                                  stop=(m == K1 - 1))
                    last.then_inc(lay2, 1)
                elif piece == "last":
                    pe.wait_ge(act2, k * K2 + K2)
                    for m in range(K2):
                        last = mm(tower_ps[0:1, :], w3[:, m:m + 1], hid2[:, m, :], start=(m == 0), stop=(m == K2 - 1))
                    last.then_inc(lay3, 1)
                else:
                    if piece == 0:
                        pe.wait_ge(zct_ready, k + 1)
                    else:
                        pe.wait_ge(act1, k * K1 + piece)
                    mm(tower_ps, w1[:, P * piece:P * piece + P], zct[:, :], start=True, stop=True).then_inc(lay1, 1)

            def tower_read(k, piece):
                if piece == "sum":
                    pe.wait_ge(ln_step, k * NORM_STEPS + 1)
                elif piece == "turn":
                    pe.wait_ge(zct_ready, k + 1)
                elif piece in ("wide0", "wide1"):
                    pe.wait_ge(act2, k * K2 + int(piece[-1]) + 1)
                elif piece == "last":
                    pe.wait_ge(y_taken, k + 1)
                else:
                    pe.wait_ge(act1, k * K1 + piece + 1)

            def chunk(k, first, last):
                for g in range(NG):
                    make_tiles(k, g, first)
                    if g >= LAG:
                        if g == LAG and first:
                            pe.wait_ge(dw_loaded, 16)
                        if g == LAG and not first:
                            pe.wait_ge(h_taken, k)
                        sum_products(k, g - LAG)
                    elif not first:
                        sum_products(k - 1, NG - LAG + g)
                    if g in HIGH_AT and (HIGH_AT[g] >= AHEAD or not last):
                        c = HIGH_AT[g]
                        take_high(k if c >= AHEAD else k + 1, c)
                    if g in TOWER_AT and not first:
                        turns = [x for x in HIGH_AT if x <= g and HIGH_AT[x] >= AHEAD]
                        pe.wait_ge(parts_ready, k * NC + (HIGH_AT[max(turns)] + 1))
                        tower(k - 1, TOWER_AT[g])
                    if g in TURN_AT and (TURN_AT[g] >= AHEAD or not last):
                        c = TURN_AT[g]
                        pieces = [x for x in TOWER_AT if x <= g]
                        if pieces and not first:
                            tower_read(k - 1, TOWER_AT[max(pieces)])
                        if c >= LOOKED:
                            turn(k if c >= AHEAD else k + 1, c, False)
                    if g in LOOK_AT and not last:
                        look_up(k + 1, *LOOK_AT[g], False)

            pe.wait_ge(ident_loaded, 16)
            pe.wait_ge(neg_made, 1)
            pe.wait_ge(zc_filled, 2)
            pe.wait_ge(h_cleared, 1)
            for c in range(AHEAD):
                if c < LOOKED:
                    for t in range(KT):
                        look_up(0, c, t, True)
                else:
                    turn(0, c, False)
                take_high(0, c)
            chunk(0, True, False)
            pe.wait_ge(consts_in, 16 * 6)
            with pe.Fori(1, NCH - 1) as k:
                chunk(k, False, False)
            chunk(NCH - 1, False, True)
            for g in range(NG - LAG, NG):
                sum_products(NCH - 1, g)
            pe.wait_ge(h_taken, NCH)
            for piece in TOWER_AT.values():
                tower(NCH - 1, piece)


def kernel(**inputs):
    import numpy as np
    import concourse.bacc as bacc
    from concourse import mybir as mb
    from concourse.bass_utils import run_bass_kernel_spmd as run

    a = {n: np.ascontiguousarray(v) for n, v in inputs.items()}
    ids = a["ids"][:, ORDER[LOOKED * R:]].reshape(NCH, BT, P, FETCHED * R).transpose(2, 0, 3, 1)
    W, dense_w = a["L0_rec_W"], a["L0_rec_dense_w"]
    w_tiles = np.zeros((E, NT, R, E), W.dtype)
    dw_tiles = np.zeros((R, E, NT, D), dense_w.dtype)
    pair = 0
    place = {f: n for n, f in enumerate(ORDER)}
    for f in range(FIELDS):
        for g in range(f + 1, FIELDS):
            i, j = sorted((place[f], place[g]))
            tile = TILE0[STEP_START[j // R] + i // R] + i % R
            w_tiles[:, tile, j % R, :] = W[pair] if ORDER[i] == f else W[pair].T
            dw_tiles[j % R, :, tile, :] = dense_w[pair]
            pair += 1
    sel = np.zeros((P, D), np.float32)
    for g in range(R):
        sel[E * g:E * g + D] = np.eye(D, dtype=np.float32)
    rows = np.stack([a["L0_rec_dense_b"], a["L0_rec_gamma"], a["L0_rec_beta"]])
    arrays = {
        "ids": ids.reshape(P, NCH, FETCHED * R * BT),
        "small_ids": a["ids"][:, SMALL].reshape(NCH, CH, LOOKED * R).transpose(0, 2, 1).reshape(-1, CH),
        "iota": np.arange(P * KT, dtype=np.float32).reshape(P, KT),
        "dense_ctx": a["dense_ctx"].reshape(NCH, BT, P, D).transpose(0, 2, 1, 3),
        "W": np.concatenate([w_tiles[:, t0:t1].reshape(P, (t1 - t0) * E) for t0, t1 in W_TILES], axis=1),
        "dense_w": dw_tiles.reshape(P, NT, D),
        "w1": np.concatenate([a["W_top1"], a["b_top1"][None]]),
        "w2": a["W_top2"].reshape(K1, P, H2).transpose(1, 0, 2),
        "w3": a["W_top3"].reshape(K2, P).T,
        "b2": a["b_top2"].reshape(K2, P).T,
        "rows": np.broadcast_to(rows[None], (P, 3, D)),
        "ident": np.eye(P, dtype=np.float32),
        "sel": sel,
    }
    for f in range(FIELDS):
        arrays[f"tbl_{f}"] = a[f"tbl_{f}"]
    arrays = {f"in_{n}": np.ascontiguousarray(v) for n, v in arrays.items()}

    nc = bacc.Bacc("TRN2", target_bir_lowering=False, num_devices=1)
    args = [nc.dram_tensor(n, v.shape, mb.dt.from_np(v.dtype), kind="ExternalInput").ap() for n, v in arrays.items()]
    out = nc.dram_tensor("out_y", (BATCH, 1), F32, kind="ExternalOutput").ap()
    build(nc, *args, out)
    r = run(nc, [arrays], core_ids=[0])
    return r.results[0]["out_y"]
```

```python
from contextlib import ExitStack

import concourse.bass as bass
from concourse import mybir

F32 = mybir.dt.float32
F32R = mybir.dt.float32r
F16 = mybir.dt.float16
BF16 = mybir.dt.bfloat16
I32 = mybir.dt.int32
ALU = mybir.AluOpType
ACT = mybir.ActivationFunctionType
AX_X = mybir.AxisListType.X

P = 128
BATCH = 2048
FIELDS = 40
E = 32
D = 16
CH = 256
NCH = BATCH // CH
BT = CH // P
R = P // E
NC = FIELDS // R
H1, H2 = 512, 256
K1 = H1 // P
K2 = H2 // P
LN_EPS = 1e-3

GROUPS = [(c, a, R if a < c else R - 1) for c in range(NC) for a in range(c + 1)]
NG = len(GROUPS)
TILE0 = [sum(n for _, _, n in GROUPS[:g]) for g in range(NG + 1)]
NT = TILE0[-1]
STEP_START = [c * (c + 1) // 2 for c in range(NC + 1)]

SMALL = (5, 10, 11, 14)
ORDER = SMALL + tuple(f for f in range(FIELDS) if f not in SMALL)
TABLE = 1000
KT = 8
KP = TABLE // KT
FETCHED = NC - 1

SLOTS = 3
SLOT = [g % SLOTS for g in range(NG - 1)] + [1]
XT_SLOT = [0, 1, 2, 3, 0, 1, 2, 0, 2, 3]
XT_SLOTS = max(XT_SLOT) + 1
ROW_SLOT = [0, 1, 2, 3, 4, 0, 1, 2, 3]
ROW_SLOTS = max(ROW_SLOT) + 1
LAG = 2

W_PIECES = [(0, 3), (3, 5), (5, 7), (7, 9), (9, 10)]
W_TILES = [(TILE0[STEP_START[c0]], TILE0[STEP_START[c1]]) for c0, c1 in W_PIECES]

DOUBLE_AT = {8: 5, 13: 6, 18: 7, 25: 8, 32: 9}

LOOK_AT = {36 + t: t for t in range(KT)}
MASK_AT = {g - 1: t for g, t in LOOK_AT.items()}
TURN_AT = {43: 0, 46: 1, 49: 2, 1: 3, 4: 4, 10: 5, 17: 6, 22: 7, 29: 8, 34: 9}
HIGH_AT = {44: 0, 47: 1, 50: 2, 2: 3, 5: 4, 11: 5, 18: 6, 23: 7, 30: 8, 35: 9}
AHEAD = 3
TOWER_AT = {7: "sum", 14: "turn", 15: 0, 16: 1, 20: 2, 21: 3, 25: "half0", 26: "wide0", 27: "half1", 28: "wide1",
            31: "last"}
NORM_AT = {7: (0,), 8: (1, 2), 9: (3, 4), 10: (5, 6), 12: (7, 8), 13: (9,)}
ROOT_AT = 11


def last_in_slot(g):
    before = [x for x in range(g) if SLOT[x] == SLOT[g]]
    return before[-1] if before else max(x for x in range(NG) if SLOT[x] == SLOT[g]) - NG


def build(nc, ids, small_ids, iota_in, ctx_in, W_in, dw_in, w1_in, w2_in, w3_in, b2_in, rows_in, ident_in, sel_in,
          *rest):
    tables, out = rest[:FIELDS], rest[FIELDS]

    with ExitStack() as ctx:
        def sb(name, shape, dt):
            return ctx.enter_context(nc.sbuf_tensor(name, shape, dt))

        def sem(name):
            return ctx.enter_context(nc.semaphore(name))

        w_a = sb("w_a", [P, NT * P], F32R)
        x_a = sb("x_a", [P, NC, R, CH], F32R)
        dw = sb("dw", [P, NT, D], F32)
        q_buf = sb("q_buf", [P, SLOTS, R, CH], F32)
        xt = sb("xt", [P, XT_SLOTS, CH], F32)
        rows = sb("rows", [P, ROW_SLOTS, BT, P], F32)
        parts = sb("parts", [P, 2, 2, CH], F32R)
        ids_all = sb("ids_all", [P, NCH, FETCHED * R * BT], I32)
        look_w = sb("look_w", [P, KT, 3, P], BF16)
        iota = sb("iota", [P, KT], F32)
        ident = sb("ident", [P, P], F32)
        neg_ident = sb("neg_ident", [P, P], F32R)
        sel = sb("sel", [P, D], F32)
        w1 = sb("w1", [P, H1], F32)
        w2 = sb("w2", [P, K1, H2], F32)
        w3 = sb("w3", [P, K2], F32)
        b2 = sb("b2", [P, K2], F32)
        row_consts = sb("row_consts", [P, 3, D], F32)
        h_sb = sb("h_sb", [P, BT, D], F32)
        sq = sb("sq", [P, BT, D], F32)
        stat = sb("stat", [P, 3, BT], F32)
        zc = sb("zc", [P, BT, P], F32)
        zct = sb("zct", [P, CH], F32)
        hid1 = sb("hid1", [P, K1, CH], F32)
        hid2 = sb("hid2", [P, K2, CH], F32)
        h_parts = hid2[:, 0, :]
        y_sb = zct[0:1, :]
        masks = hid1[:, :, :].rearrange("p k b -> p (k b)").bitcast(BF16).rearrange("p (s c) -> p s c", s=2)
        ids16 = hid2[:, :, :].rearrange("p k b -> p (k b)").bitcast(F16)
        raw_tables = hid1[0:KP, :, :].rearrange("p k b -> p (k b)").rearrange("p (r t e) -> p r t e", r=R, t=KT)
        raw_ids = xt[0:NCH * R, 0, :].bitcast(I32)
        part_ids = xt[0:NCH * R, 1, 0:CH // 2].bitcast(F16)
        flat_q = q_buf[:, :, :, :].rearrange("p g r b -> p (g r b)")
        flat_dw = dw[:, :, :].rearrange("p t d -> p (t d)")
        w_raw = []
        for n, (t0, t1) in enumerate(W_TILES):
            room, start = (flat_dw, t0) if n in (2, 3) else (flat_q, t0 - W_TILES[1][1] if n == 4 else 0)
            w_raw.append(room[:, (t0 - start) * E:(t1 - start) * E])
        behind_x = x_a[:, NC // 2:, :, :].rearrange("p c r b -> p (c r b)")
        w_stage = []
        for n, (t0, t1) in enumerate(W_TILES):
            start = {3: 0, 4: W_TILES[3][0] * P}.get(n, NT * P - 2 * (W_TILES[2][1] - t0) * E)
            room = behind_x if n == 3 else w_a
            w_stage.append(room[:, start:start + 2 * (t1 - t0) * E].rearrange("p (s c) -> p s c", s=2))

        t_ps = ctx.enter_context(nc.psum_tensor("t_ps", [P, SLOTS, R, CH], F32))
        side_ps = ctx.enter_context(nc.psum_tensor("side_ps", [P, 2, CH], F32))
        h_ps = ctx.enter_context(nc.psum_tensor("h_ps", [P, CH], F32))
        turn_ps = side_ps[:, 0, :]
        tower_ps = side_ps[:, 1, :]

        ids_small = nc.dram_tensor("ids_small", [NCH, R * CH], F16, kind="Internal").ap()
        x_spill = nc.dram_tensor("x_spill", [2, 2, E, R, CH], F32, kind="Internal").ap()

        ids_in = sem("ids_in")
        consts_in = sem("consts_in")
        ident_loaded, dw_loaded = sem("ident_loaded"), sem("dw_loaded")
        raw_in = [sem(f"raw_in{n}") for n in range(len(W_PIECES))]
        w_high_ready, w_split = sem("w_high_ready"), sem("w_split")
        w_top_ready, w_low_ready = sem("w_top_ready"), sem("w_low_ready")
        w_in = [sem(f"w_in{n}") for n in range(len(W_PIECES))]
        neg_made, zc_filled, h_cleared = sem("neg_made"), sem("zc_filled"), sem("h_cleared")
        tables_in = sem("tables_in")
        tables_high, tables_rest, tables_mid = sem("tables_high"), sem("tables_rest"), sem("tables_mid")
        tables_low = sem("tables_low")
        iota_loaded, small_in, small_ready, small_out = (sem("iota_loaded"), sem("small_in"), sem("small_ready"),
                                                         sem("small_out"))
        ids16_loaded, mask_ready, looked_up = sem("ids16_loaded"), sem("mask_ready"), sem("looked_up")
        gathered = [sem(f"gathered{n}") for n in range(ROW_SLOTS)]
        turned, xt_ready, high_ready = sem("turned"), sem("xt_ready"), sem("high_ready")
        less_high, parts_ready = sem("less_high"), sem("parts_ready")
        spilled = [sem(f"spilled{n}") for n in range(2)]
        x_stacked = [sem(f"x_stacked{n}") for n in range(2)]
        t_ready, multiplied, summed = sem("t_ready"), sem("multiplied"), sem("summed")
        h_taken, sum_ready = sem("h_taken"), sem("sum_ready")
        ln_step, var_ready, dev_ready, z_ready = sem("ln_step"), sem("var_ready"), sem("dev_ready"), sem("z_ready")
        ctx_loaded, z_turned, zct_ready = sem("ctx_loaded"), sem("z_turned"), sem("zct_ready")
        lay1, act1, lay2, act2, lay3 = sem("lay1"), sem("act1"), sem("lay2"), sem("act2"), sem("lay3")
        y_taken, y_stored = sem("y_taken"), sem("y_stored")

        block = ctx.enter_context(nc.Block())

        NORM_STEPS = 8
        GATHERS = R * BT * 16

        def split_tables(s):
            return look_w[0:KP, :, s, :].rearrange("p t (r e) -> p r t e", r=R)

        @block.sync
        def _(sp):
            def load_ctx(k):
                sp.dma_start(zc[:, :, D:2 * D], ctx_in[k]).then_inc(ctx_loaded, 16)

            def store_y(k):
                sp.wait_ge(y_taken, k + 1)
                sp.dma_start(out[k * CH:(k + 1) * CH, :].rearrange("b o -> o b"), y_sb).then_inc(y_stored, 16)

            def send_block(k, c):
                m, n = c % 2, k * NC + c
                sp.wait_ge(parts_ready, n + 1)
                if n >= 2:
                    sp.wait_ge(x_stacked[m], 32 * (n // 2))
                for r in range(R):
                    sp.dma_start(x_spill[m, :, :, r, :].rearrange("s e b -> e s b"),
                                 parts[E * r:E * r + E, m, :, :].bitcast(F32)).then_inc(spilled[m], 16)

            def stack_block(k, c):
                m, n = c % 2, k * NC + c
                sp.wait_ge(spilled[m], R * 16 * (n // 2 + 1))
                if k:
                    last_use = STEP_START[NC - 1] + c
                    sp.wait_ge(multiplied, (k - 1) * NG + last_use + 1)
                for half in range(2):
                    sp.dma_start(x_a[64 * half:64 * half + 64, c, :, :].bitcast(F32),
                                 x_spill[m].rearrange("s e r b -> (s e) r b")).then_inc(x_stacked[m], 16)

            def load_ids16(k):
                if k:
                    sp.wait_ge(mask_ready, k * KT)
                if k > 1:
                    sp.wait_ge(lay3, k - 1)
                sp.dma_start(ids16, ids_small[k:k + 1, :].to_broadcast([P, R * CH])).then_inc(ids16_loaded, 16)

            sp.dma_start(ids_all[:, :, :], ids).then_inc(ids_in, 16)
            sp.dma_start(raw_ids, small_ids).then_inc(small_in, 16)
            for r in range(R):
                sp.dma_start(hid1[0:KP, r, :], tables[ORDER[r]].rearrange("(p t) e -> p (t e)", t=KT))\
                  .then_inc(tables_in, 16)
            sp.dma_start(iota[:, :], iota_in).then_inc(iota_loaded, 16)
            sp.dma_start(ident[:, :], ident_in).then_inc(ident_loaded, 16)
            def load_raw(n):
                t0, t1 = W_TILES[n]
                sp.dma_start(w_raw[n], W_in[:, t0 * E:t1 * E]).then_inc(raw_in[n], 16)

            def load_w(n):
                t0, t1 = W_TILES[n]
                sp.wait_ge(w_split, n + 1)
                if n >= 3:
                    for m in (0, 1, 2, 4)[:n + 1 if n == 3 else 3]:
                        sp.wait_ge(w_in[m], 128)
                size = (t1 - t0) * E
                for q in range(P // E):
                    for part in range(2):
                        sp.dma_start(w_a[64 * part:64 * part + E, t0 * P + q * size:t0 * P + (q + 1) * size].bitcast(F32),
                                     w_stage[n][E * q:E * q + E, part, :].bitcast(F32)).then_inc(w_in[n], 16)

            def load_consts():
                for dst, src in ((sel, sel_in), (w1, w1_in), (w3, w3_in), (b2, b2_in)):
                    sp.dma_start(dst[:, :], src).then_inc(consts_in, 16)
                for dst, src in ((w2, w2_in), (row_consts, rows_in)):
                    sp.dma_start(dst[:, :, :], src).then_inc(consts_in, 16)

            for n in (0, 1, 2, 4):
                load_raw(n)
            sp.wait_ge(small_ready, 1)
            sp.dma_start(ids_small.rearrange("n (r b) -> (n r) b", r=R), part_ids).then_inc(small_out, 16)
            sp.wait_ge(small_out, 16)
            load_ids16(0)
            load_w(0)
            sp.wait_ge(w_split, 3)
            load_raw(3)
            load_w(1)
            send_block(0, 0)
            stack_block(0, 0)
            send_block(0, 1)
            sp.wait_ge(w_split, 4)
            sp.dma_start(dw[:, :, :], dw_in).then_inc(dw_loaded, 16)
            stack_block(0, 1)
            load_w(2)
            send_block(0, 2)
            stack_block(0, 2)
            for k in range(NCH):
                for c in range(NC):
                    if c >= AHEAD:
                        send_block(k, c)
                        if c == 8 and k:
                            store_y(k - 1)
                        if c == 8 and k + 1 < NCH:
                            load_ids16(k + 1)
                        if k == 0 and c == NC // 2:
                            sp.wait_ge(w_in[3], 128)
                        stack_block(k, c)
                        if k == 0 and c == 3:
                            load_w(4)
                        if k == 0 and c == 4:
                            load_w(3)
                        if k == 0 and c == 7:
                            load_consts()
                            load_ctx(0)
                if k:
                    sp.wait_ge(y_stored, 16 * k)
                    load_ctx(k)
                if k + 1 < NCH:
                    send_block(k + 1, 0)
                    stack_block(k + 1, 0)
                    send_block(k + 1, 1)
                    send_block(k + 1, 2)
                    stack_block(k + 1, 1)
                    stack_block(k + 1, 2)
            store_y(NCH - 1)
            sp.wait_ge(y_stored, 16 * NCH)

        @block.gpsimd
        def _(pool):
            pool.wait_ge(ids_in, 16)
            for k in range(NCH):
                for j in range(FETCHED):
                    slot = ROW_SLOT[j]
                    before = [x for x in range(k * FETCHED + j) if ROW_SLOT[x % FETCHED] == slot]
                    if before:
                        pool.wait_ge(turned, before[-1] + 1)
                    for r in range(R):
                        for t in range(BT):
                            i = (R * j + r) * BT + t
                            pool.indirect_dma_start(
                                rows[:, slot, t, E * r:E * r + E], None, tables[ORDER[R * (j + 1) + r]],
                                bass.IndirectOffsetOnAxis(ids_all[:, k, i:i + 1], 0))\
                                .then_inc(gathered[slot], 16)
            for m in range(ROW_SLOTS):
                pool.wait_ge(gathered[m], NCH * ROW_SLOT.count(m) * GATHERS)

        @block.scalar
        def _(act):
            copy = ACT.Copy

            def first_parts(k, c, first):
                if c == 0:
                    act.wait_ge(looked_up, k * KT + KT)
                else:
                    act.wait_ge(turned, k * FETCHED + c)
                before = [x for x in range(c) if XT_SLOT[x] == XT_SLOT[c]]
                if before:
                    act.wait_ge(multiplied, k * NG + STEP_START[before[-1] + 1])
                elif not first:
                    step = max(x for x in range(NC) if XT_SLOT[x] == XT_SLOT[c])
                    act.wait_ge(multiplied, k * NG - NG + STEP_START[step + 1])
                nc.scalar.activation(xt[:, XT_SLOT[c], :], turn_ps, copy).then_inc(xt_ready, 1)
                if not first or c >= 2:
                    act.wait_ge(spilled[c % 2], k * (NC // 2 * R * 16) + R * 16 * (c // 2))
                nc.scalar.activation(parts[:, c % 2, 0, :], turn_ps, copy).then_inc(high_ready, 1)

            def low_part(k, c):
                act.wait_ge(less_high, k * NC + c + 1)
                nc.scalar.activation(parts[:, c % 2, 1, :], turn_ps, copy).then_inc(parts_ready, 1)

            def split_w(n):
                act.wait_ge(raw_in[n], 16)
                nc.scalar.activation(w_stage[n][:, 0, :], w_raw[n], copy).then_inc(w_high_ready, 1)

            def double_w(c):
                cols = slice(TILE0[STEP_START[c]] * P, TILE0[STEP_START[c + 1]] * P)
                for n, (c0, c1) in enumerate(W_PIECES):
                    if c0 == c:
                        act.wait_ge(w_in[n], 128)
                nc.scalar.activation(w_a[E:2 * E, cols], w_a[0:E, cols].bitcast(F32), copy).then_inc(w_top_ready, 1)

            def take_h(k):
                act.wait_ge(summed, k * NG + NG)
                nc.scalar.activation(h_parts, h_ps[:, :], copy).then_inc(h_taken, 1)

            def tower(k, piece):
                if piece == "turn":
                    act.wait_ge(z_turned, k + 1)
                    act.wait_ge(ctx_loaded, k * 16 + 16)
                    nc.scalar.activation(zct[:, :], tower_ps, copy).then_inc(zct_ready, 1)
                elif piece == "last":
                    act.wait_ge(lay3, k + 1)
                    nc.scalar.activation(y_sb, tower_ps[0:1, :], copy).then_inc(y_taken, 1)
                elif piece in ("wide0", "wide1"):
                    n = int(piece[-1])
                    act.wait_ge(lay2, k * K2 + n + 1)
                    nc.scalar.activation(hid2[:, n, :], tower_ps, ACT.Relu, bias=b2[:, n:n + 1]).then_inc(act2, 1)
                elif piece not in ("sum", "half0", "half1"):
                    act.wait_ge(lay1, k * K1 + piece + 1)
                    nc.scalar.activation(hid1[:, piece, :], tower_ps, ACT.Relu).then_inc(act1, 1)

            def root(k):
                act.wait_ge(var_ready, k + 1)
                nc.scalar.activation(stat[:, 1, :], stat[:, 1, :], ACT.Sqrt).then_inc(dev_ready, 1)

            def chunk(k, first, last):
                for g in range(NG):
                    if g == LAG - 1 and not first:
                        take_h(k - 1)
                    if g in HIGH_AT and (HIGH_AT[g] >= AHEAD or not last):
                        c = HIGH_AT[g]
                        low_part(k if c >= AHEAD else k + 1, c)
                    if g in TOWER_AT and not first:
                        tower(k - 1, TOWER_AT[g])
                    if g == ROOT_AT and not first:
                        root(k - 1)
                    if g in TURN_AT and (TURN_AT[g] >= AHEAD or not last):
                        c = TURN_AT[g]
                        first_parts(k if c >= AHEAD else k + 1, c, first and c >= AHEAD)
                    if g in DOUBLE_AT and first:
                        double_w(DOUBLE_AT[g])

            act.wait_ge(ident_loaded, 16)
            nc.scalar.activation(neg_ident[:, :], ident[:, :], copy, scale=-1.0).then_inc(neg_made, 1)
            act.wait_ge(small_in, 16)
            nc.scalar.activation(part_ids, raw_ids, copy).then_inc(small_ready, 1)
            act.wait_ge(tables_in, R * 16)
            nc.scalar.activation(split_tables(0), raw_tables, copy).then_inc(tables_high, 1)
            split_w(0)
            act.wait_ge(tables_rest, 1)
            nc.scalar.activation(split_tables(1), raw_tables, copy).then_inc(tables_mid, 1)
            for n in range(1, len(W_PIECES)):
                split_w(n)
            for c in range(AHEAD):
                first_parts(0, c, True)
                low_part(0, c)
                for step in ((0, 1, 2), (3,), (4,))[c]:
                    double_w(step)
            chunk(0, True, False)
            act.wait_ge(consts_in, 16 * 6)
            with act.Fori(1, NCH - 1) as k:
                chunk(k, False, False)
            chunk(NCH - 1, False, True)
            take_h(NCH - 1)
            root(NCH - 1)
            for piece in TOWER_AT.values():
                tower(NCH - 1, piece)

        @block.vector
        def _(dve):
            def split_w(n):
                dve.wait_ge(w_high_ready, n + 1)
                nc.vector.tensor_tensor(w_stage[n][:, 1, :], w_raw[n], w_stage[n][:, 0, :].bitcast(F32),
                                        ALU.subtract).then_inc(w_split, 1)

            def double_w(c):
                cols = slice(TILE0[STEP_START[c]] * P, TILE0[STEP_START[c + 1]] * P)
                for n, (c0, c1) in enumerate(W_PIECES):
                    if c0 == c:
                        dve.wait_ge(w_in[n], 128)
                nc.vector.tensor_copy(w_a[96:P, cols], w_a[64:96, cols].bitcast(F32)).then_inc(w_low_ready, 1)

            def multiply(k, g, first):
                c, _, n = GROUPS[g]
                if g == STEP_START[c]:
                    dve.wait_ge(xt_ready, k * NC + c + 1)
                if not first or g >= SLOTS:
                    dve.wait_ge(summed, k * NG + last_in_slot(g) + 1)
                dve.wait_ge(t_ready, k * NG + g + 1)
                x = xt[:, XT_SLOT[c], :].unsqueeze(1).to_broadcast([P, n, CH])
                nc.vector.tensor_tensor(q_buf[:, SLOT[g], 0:n, :], t_ps[:, SLOT[g], 0:n, :], x,
                                        ALU.mult).then_inc(multiplied, 1)

            def wide(ap):
                return ap.unsqueeze(2).to_broadcast([P, BT, D])

            def const(n):
                return row_consts[:, n, :].unsqueeze(1).to_broadcast([P, BT, D])

            def norm(k, n):
                def after(count):
                    dve.wait_ge(ln_step, k * NORM_STEPS + count)

                v = nc.vector
                total, var, inv = stat[:, 0, :], stat[:, 1, :], stat[:, 2, :]
                if n == 0:
                    dve.wait_ge(sum_ready, k + 1)
                    h = tower_ps[:, 0:BT * D].rearrange("p (t d) -> p t d", t=BT)
                    v.tensor_tensor(h_sb[:, :, :], h, const(0), ALU.add).then_inc(ln_step, 1)
                elif n == 1:
                    after(1)
                    v.tensor_reduce(total, h_sb[:, :, :], AX_X, ALU.add).then_inc(ln_step, 1)
                elif n == 2:
                    after(2)
                    v.tensor_scalar(total, total, 1.0 / D, None, ALU.mult).then_inc(ln_step, 1)
                elif n == 3:
                    after(3)
                    v.tensor_tensor(h_sb[:, :, :], h_sb[:, :, :], wide(total), ALU.subtract).then_inc(ln_step, 1)
                elif n == 4:
                    after(4)
                    v.tensor_tensor(sq[:, :, :], h_sb[:, :, :], h_sb[:, :, :], ALU.mult).then_inc(ln_step, 1)
                elif n == 5:
                    after(5)
                    v.tensor_reduce(var, sq[:, :, :], AX_X, ALU.add).then_inc(ln_step, 1)
                elif n == 6:
                    after(6)
                    v.tensor_scalar(var, var, 1.0 / D, LN_EPS, ALU.mult, ALU.add).then_inc(var_ready, 1)
                elif n == 7:
                    v.tensor_tensor(sq[:, :, :], h_sb[:, :, :], const(1), ALU.mult).then_inc(ln_step, 1)
                    dve.wait_ge(dev_ready, k + 1)
                    v.reciprocal(inv, var).then_inc(ln_step, 1)
                elif n == 8:
                    after(NORM_STEPS)
                    v.tensor_tensor(h_sb[:, :, :], sq[:, :, :], wide(inv), ALU.mult).then_inc(z_ready, 1)
                elif n == 9:
                    dve.wait_ge(z_ready, 2 * k + 1)
                    v.tensor_tensor(zc[:, :, 0:D], h_sb[:, :, :], const(2), ALU.add).then_inc(z_ready, 1)

            def make_mask(k, t):
                n = k * KT + t
                if t == 0:
                    dve.wait_ge(ids16_loaded, k * 16 + 16)
                if not isinstance(n, int) or n >= 2:
                    dve.wait_ge(looked_up, n - 1)
                nc.vector.tensor_scalar(masks[0:KP, t % 2, :], ids16[0:KP, :], iota[0:KP, t:t + 1], None,
                                        ALU.is_equal).then_inc(mask_ready, 1)

            def chunk(k, first, last):
                for g in range(NG):
                    multiply(k, g, first)
                    if not first:
                        for n in NORM_AT.get(g, ()):
                            norm(k - 1, n)
                    if g in MASK_AT and not last:
                        make_mask(k + 1, MASK_AT[g])
                    if g in DOUBLE_AT and first:
                        double_w(DOUBLE_AT[g])

            nc.vector.memset(h_ps[:, :], 0.0).then_inc(h_cleared, 1)
            nc.vector.memset(zc[:, :, E:E + 1], 1.0).then_inc(zc_filled, 1)
            nc.vector.memset(zc[:, :, E + 1:P], 0.0).then_inc(zc_filled, 1)
            dve.wait_ge(tables_high, 1)
            nc.vector.tensor_tensor(raw_tables, raw_tables, split_tables(0), ALU.subtract).then_inc(tables_rest, 1)
            split_w(0)
            dve.wait_ge(tables_mid, 1)
            nc.vector.tensor_tensor(split_tables(2), raw_tables, split_tables(1), ALU.subtract).then_inc(tables_low, 1)
            split_w(1)
            split_w(2)
            dve.wait_ge(iota_loaded, 16)
            dve.wait_ge(tables_low, 1)
            for t in range(KT):
                make_mask(0, t)
                if t in (2, 4):
                    split_w(2 + t // 2)
            for step in range(3):
                double_w(step)
            for step in range(3, 5):
                double_w(step)
            chunk(0, True, False)
            dve.wait_ge(consts_in, 16 * 6)
            with dve.Fori(1, NCH - 1) as k:
                chunk(k, False, False)
            chunk(NCH - 1, False, True)
            for n in range(10):
                norm(NCH - 1, n)

        @block.tensor
        def _(pe):
            mm = nc.tensor.matmul

            def turn(k, c, first):
                slot = ROW_SLOT[c - 1]
                uses = ROW_SLOT.count(slot), ROW_SLOT[:c].count(slot)
                pe.wait_ge(gathered[slot], k * (uses[0] * GATHERS) + uses[1] * GATHERS)
                if not first or c >= 1:
                    pe.wait_ge(parts_ready, k * NC + c)
                for t in range(BT):
                    last = mm(turn_ps[:, P * t:P * t + P], rows[:, slot, t, :], ident[:, :],
                              is_transpose=True, start=(t == 0), stop=False, skip_group_check=True)
                last.then_inc(turned, 1)

            def look_up(k, t, first):
                if t == 0 and not first:
                    pe.wait_ge(parts_ready, k * NC)
                if first:
                    pe.wait_ge(tables_low, 1)
                pe.wait_ge(mask_ready, k * KT + t + 1)
                for s in range(3):
                    for r in range(R):
                        last = mm(turn_ps[E * r:E * r + E, :], look_w[0:KP, t, s, E * r:E * r + E],
                                  masks[0:KP, t % 2, CH * r:CH * r + CH], start=(t == 0 and s == 0), stop=False,
                                  skip_group_check=True)
                last.then_inc(looked_up, 1)

            def take_high(k, c):
                pe.wait_ge(xt_ready, k * NC + c + 1)
                pe.wait_ge(high_ready, k * NC + c + 1)
                mm(turn_ps, neg_ident[:, :], parts[:, c % 2, 0, :], start=False, stop=True,
                   skip_group_check=True).then_inc(less_high, 1)

            def make_tiles(k, g, first):
                c, a, n = GROUPS[g]
                if not first or g >= SLOTS:
                    pe.wait_ge(multiplied, k * NG + last_in_slot(g) + 1)
                if first and a == 0:
                    pe.wait_ge(w_top_ready, c + 1)
                    pe.wait_ge(w_low_ready, c + 1)
                if a == c:
                    pe.wait_ge(x_stacked[c % 2], k * (NC // 2 * 32) + 32 * (c // 2 + 1))
                for r in range(n):
                    tile = TILE0[g] + r
                    last = mm(t_ps[:, SLOT[g], r, :], w_a[:, tile * P:tile * P + P], x_a[:, a, r, :],
                              start=True, stop=True)
                last.then_inc(t_ready, 1)

            def sum_products(k, g):
                pe.wait_ge(multiplied, k * NG + g + 1)
                for r in range(GROUPS[g][2]):
                    last = mm(h_ps[E * r:E * r + D, :], dw[:, TILE0[g] + r, :], q_buf[:, SLOT[g], r, :],
                              start=(g == 0 or (g == 1 and r == R - 1)), stop=(g >= NG - 2),
                              skip_group_check=True)
                last.then_inc(summed, 1)

            def tower(k, piece):
                if piece == "sum":
                    for t in range(BT):
                        last = mm(tower_ps[:, D * t:D * t + D], h_parts[:, P * t:P * t + P], sel[:, :],
                                  start=(t == 0), stop=(t == BT - 1), skip_group_check=True)
                    last.then_inc(sum_ready, 1)
                elif piece == "turn":
                    pe.wait_ge(z_ready, 2 * k + 2)
                    pe.wait_ge(ctx_loaded, k * 16 + 16)
                    for t in range(BT):
                        last = mm(tower_ps[:, P * t:P * t + P], zc[:, t, :], ident[:, :], is_transpose=True,
                                  start=(t == 0), stop=(t == BT - 1), skip_group_check=True)
                    last.then_inc(z_turned, 1)
                elif piece in ("half0", "half1", "wide0", "wide1"):
                    n, half = int(piece[-1]), piece[:-1] == "half"
                    if half and n == 0:
                        pe.wait_ge(act1, k * K1 + K1)
                    elif half:
                        pe.wait_ge(act2, k * K2 + n)
                    for m in range(0, K1 // 2) if half else range(K1 // 2, K1):
                        last = mm(tower_ps, w2[:, m, P * n:P * n + P], hid1[:, m, :], start=(m == 0),
                                  stop=(m == K1 - 1))
                    if not half:
                        last.then_inc(lay2, 1)
                elif piece == "last":
                    pe.wait_ge(act2, k * K2 + K2)
                    for m in range(K2):
                        last = mm(tower_ps[0:1, :], w3[:, m:m + 1], hid2[:, m, :], start=(m == 0), stop=(m == K2 - 1))
                    last.then_inc(lay3, 1)
                else:
                    if piece == 0:
                        pe.wait_ge(zct_ready, k + 1)
                    else:
                        pe.wait_ge(act1, k * K1 + piece)
                    mm(tower_ps, w1[:, P * piece:P * piece + P], zct[:, :], start=True, stop=True).then_inc(lay1, 1)

            def tower_read(k, piece):
                if piece == "sum":
                    pe.wait_ge(ln_step, k * NORM_STEPS + 1)
                elif piece == "turn":
                    pe.wait_ge(zct_ready, k + 1)
                elif piece in ("wide0", "wide1"):
                    pe.wait_ge(act2, k * K2 + int(piece[-1]) + 1)
                elif piece == "last":
                    pe.wait_ge(y_taken, k + 1)
                else:
                    pe.wait_ge(act1, k * K1 + piece + 1)

            def chunk(k, first, last):
                for g in range(NG):
                    make_tiles(k, g, first)
                    if g >= LAG:
                        if g == LAG and first:
                            pe.wait_ge(dw_loaded, 16)
                        if g == LAG and not first:
                            pe.wait_ge(h_taken, k)
                        sum_products(k, g - LAG)
                    elif not first:
                        sum_products(k - 1, NG - LAG + g)
                    if g in HIGH_AT and (HIGH_AT[g] >= AHEAD or not last):
                        c = HIGH_AT[g]
                        take_high(k if c >= AHEAD else k + 1, c)
                    if g in TOWER_AT and not first:
                        turns = [x for x in HIGH_AT if x <= g and HIGH_AT[x] >= AHEAD]
                        pe.wait_ge(parts_ready, k * NC + (HIGH_AT[max(turns)] + 1))
                        tower(k - 1, TOWER_AT[g])
                    if g in TURN_AT and (TURN_AT[g] >= AHEAD or not last):
                        c = TURN_AT[g]
                        pieces = [x for x in TOWER_AT if x <= g]
                        if pieces and not first:
                            tower_read(k - 1, TOWER_AT[max(pieces)])
                        if c:
                            turn(k if c >= AHEAD else k + 1, c, False)
                    if g in LOOK_AT and not last:
                        look_up(k + 1, LOOK_AT[g], False)

            pe.wait_ge(ident_loaded, 16)
            pe.wait_ge(neg_made, 1)
            pe.wait_ge(zc_filled, 2)
            pe.wait_ge(h_cleared, 1)
            for c in range(AHEAD):
                if c == 0:
                    for t in range(KT):
                        look_up(0, t, True)
                else:
                    turn(0, c, False)
                take_high(0, c)
            chunk(0, True, False)
            pe.wait_ge(consts_in, 16 * 6)
            with pe.Fori(1, NCH - 1) as k:
                chunk(k, False, False)
            chunk(NCH - 1, False, True)
            for g in range(NG - LAG, NG):
                sum_products(NCH - 1, g)
            pe.wait_ge(h_taken, NCH)
            for piece in TOWER_AT.values():
                tower(NCH - 1, piece)


def kernel(**inputs):
    import numpy as np
    import concourse.bacc as bacc
    from concourse import mybir as mb
    from concourse.bass_utils import run_bass_kernel_spmd as run

    a = {n: np.ascontiguousarray(v) for n, v in inputs.items()}
    ids = a["ids"][:, ORDER[R:]].reshape(NCH, BT, P, FETCHED * R).transpose(2, 0, 3, 1)
    W, dense_w = a["L0_rec_W"], a["L0_rec_dense_w"]
    w_tiles = np.zeros((E, NT, R, E), W.dtype)
    dw_tiles = np.zeros((R, E, NT, D), dense_w.dtype)
    pair = 0
    place = {f: n for n, f in enumerate(ORDER)}
    for f in range(FIELDS):
        for g in range(f + 1, FIELDS):
            i, j = sorted((place[f], place[g]))
            tile = TILE0[STEP_START[j // R] + i // R] + i % R
            w_tiles[:, tile, j % R, :] = W[pair] if ORDER[i] == f else W[pair].T
            dw_tiles[j % R, :, tile, :] = dense_w[pair]
            pair += 1
    sel = np.zeros((P, D), np.float32)
    for g in range(R):
        sel[E * g:E * g + D] = np.eye(D, dtype=np.float32)
    rows = np.stack([a["L0_rec_dense_b"], a["L0_rec_gamma"], a["L0_rec_beta"]])
    arrays = {
        "ids": ids.reshape(P, NCH, FETCHED * R * BT),
        "small_ids": a["ids"][:, SMALL].reshape(NCH, CH, R).transpose(0, 2, 1).reshape(-1, CH),
        "iota": np.arange(P * KT, dtype=np.float32).reshape(P, KT),
        "dense_ctx": a["dense_ctx"].reshape(NCH, BT, P, D).transpose(0, 2, 1, 3),
        "W": np.concatenate([w_tiles[:, t0:t1].reshape(E, P // E, (t1 - t0) * E).transpose(1, 0, 2)
                             .reshape(P, (t1 - t0) * E) for t0, t1 in W_TILES], axis=1),
        "dense_w": dw_tiles.reshape(P, NT, D),
        "w1": np.concatenate([a["W_top1"], a["b_top1"][None], np.zeros((P - E - 1, H1), np.float32)]),
        "w2": a["W_top2"].reshape(K1, P, H2).transpose(1, 0, 2),
        "w3": a["W_top3"].reshape(K2, P).T,
        "b2": a["b_top2"].reshape(K2, P).T,
        "rows": np.broadcast_to(rows[None], (P, 3, D)),
        "ident": np.eye(P, dtype=np.float32),
        "sel": sel,
    }
    for f in range(FIELDS):
        arrays[f"tbl_{f}"] = a[f"tbl_{f}"]
    arrays = {f"in_{n}": np.ascontiguousarray(v) for n, v in arrays.items()}

    nc = bacc.Bacc("TRN2", target_bir_lowering=False, num_devices=1)
    args = [nc.dram_tensor(n, v.shape, mb.dt.from_np(v.dtype), kind="ExternalInput").ap() for n, v in arrays.items()]
    out = nc.dram_tensor("out_y", (BATCH, 1), F32, kind="ExternalOutput").ap()
    build(nc, *args, out)
    r = run(nc, [arrays], core_ids=[0])
    return r.results[0]["out_y"]
```
